# Optimizing a Trainium2 kernel written in Bass

```python
import numpy as np
import jax
import jax.numpy as jnp

def _softmax(x, axis=-1):
    return jax.nn.softmax(x, axis=axis)

def _gelu(x):
    return jax.nn.gelu(x, approximate=True)

def _silu(x):
    return jax.nn.silu(x)

def _sigmoid(x):
    return jax.nn.sigmoid(x)

def _layernorm(x, axis=-1, eps=1e-05):
    m = jnp.mean(x, axis=axis, keepdims=True)
    v = jnp.var(x, axis=axis, keepdims=True)
    return (x - m) / jnp.sqrt(v + eps)

def _scatter_add(tgt, idx, src, axis=0):
    return tgt.at[idx].add(src)

def _segment_sum(src, seg, n):
    return jax.ops.segment_sum(src, seg, n)
kernel_name = 'mk_xattn_seq_d2_seqx_r8_0bb942'

def setup_inputs(seed: int=0):
    np.random.seed(seed)
    _w = jnp.asarray

    def _rec_inputs():
        import jax
        import jax.numpy as jnp
        _rk = jax.random.key(seed)
        x = 7.22e-05 + 1 * jax.random.normal(jax.random.fold_in(_rk, 1), (8, 56, 512), jnp.float32)
        _lenS = 56 - jax.random.randint(jax.random.fold_in(_rk, 7), (8,), 0, max(1, 56 // 4) + 1, jnp.int32)
        _lenS2 = 1500 - jax.random.randint(jax.random.fold_in(_rk, 8), (8,), 0, max(1, 1500 // 4) + 1, jnp.int32)
        _ctx_4096P = jax.random.normal(jax.random.fold_in(_rk, 11), (8, 16, 512), jnp.float32)
        _ctx_4096c = jax.random.dirichlet(jax.random.fold_in(_rk, 511), 0.3 * jnp.ones((16,), jnp.float32), (8, 1500))
        _ctx_4096t = jnp.einsum('bsk,bkd->bsd', _ctx_4096c, _ctx_4096P)
        _ctx_4096t = _ctx_4096t * jax.lax.rsqrt(jnp.mean(jnp.square(_ctx_4096t)) + 1e-12) * 0.953939
        ctx_4096 = 4.13588e-05 + 0.999923 * (_ctx_4096t + 0.3 * jax.random.normal(jax.random.fold_in(_rk, 611), (8, 1500, 512), jnp.float32))
        _validS = jnp.arange(56)[None, :] < _lenS[:, None]
        _validS2 = jnp.arange(1500)[None, :] < _lenS2[:, None]
        _causal = jnp.tril(jnp.ones((56, 56), dtype=bool))
        mask_BxS2_ik0 = jnp.where(jnp.broadcast_to(_validS2[:, :], (8, 1500)), 0, 1).astype(jnp.int32)
        mask_BxS2_bf1 = jnp.ones((8, 1500), dtype=bool)
        return (x, ctx_4096, mask_BxS2_ik0, mask_BxS2_bf1)
    x, ctx_4096, mask_BxS2_ik0, mask_BxS2_bf1 = _rec_inputs()

    def _L0_xattn_setup():
        import jax, jax.numpy as jnp
        import numpy as np
        H = 512
        NH = 32
        HD = H // NH
        key = jax.random.key(seed)
        ks = jax.random.split(key, 12)
        B, L, V = (2, 128, 128)
        s = 1.0 / np.sqrt(H)
        return {'hidden_states': jax.random.normal(ks[0], (B, L, H), jnp.float32), 'vision_features': jax.random.normal(ks[1], (B, V, H), jnp.float32), 'attention_mask': jax.random.randint(ks[2], (B, V), 0, 2, jnp.int32), 'Wq': jax.random.normal(ks[3], (H, H), jnp.float32) * s, 'bq': jnp.zeros((H,), jnp.float32), 'Wk': jax.random.normal(ks[4], (H, H), jnp.float32) * s, 'bk': jnp.zeros((H,), jnp.float32), 'Wv': jax.random.normal(ks[5], (H, H), jnp.float32) * s, 'bv': jnp.zeros((H,), jnp.float32), 'Wo': jax.random.normal(ks[6], (H, H), jnp.float32) * s, 'bo': jnp.zeros((H,), jnp.float32), 'ln_g': jnp.ones((H,), jnp.float32), 'ln_b': jnp.zeros((H,), jnp.float32)}
    _L0_xattn_all = _L0_xattn_setup()
    _L0_xattn_in = {k: v for k, v in _L0_xattn_all.items() if k in ('Wq', 'bq', 'Wk', 'bk', 'Wv', 'bv', 'Wo', 'bo', 'ln_g', 'ln_b')}
    del _L0_xattn_all

    def _L1_xattn_setup():
        import jax, jax.numpy as jnp
        import numpy as np
        HIDDEN = 512
        HEADS = 32
        HEAD_DIM = HIDDEN // HEADS
        LN_EPS = 1e-05

        def _split_heads(x):
            B, S, _ = x.shape
            return x.reshape(B, S, HEADS, HEAD_DIM).transpose(0, 2, 1, 3)
        key = jax.random.key(seed)
        ks = jax.random.split(key, 7)
        B, S, SLOTS = (2, 512, 128)
        hidden_states = jax.random.normal(ks[0], (B, S, HIDDEN), dtype=jnp.float32)
        memory_keys = jax.random.normal(ks[1], (B, SLOTS, HIDDEN), dtype=jnp.float32)
        memory_values = jax.random.normal(ks[2], (B, SLOTS, HIDDEN), dtype=jnp.float32)
        attention_mask = jnp.ones((B, SLOTS), dtype=jnp.bool_)
        Wq = jax.random.normal(ks[3], (HIDDEN, HIDDEN), dtype=jnp.float32) / np.sqrt(HIDDEN)
        Wout = jax.random.normal(ks[4], (HIDDEN, HIDDEN), dtype=jnp.float32) / np.sqrt(HIDDEN)
        ln_gamma = jnp.ones((HIDDEN,), dtype=jnp.float32)
        ln_beta = jnp.zeros((HIDDEN,), dtype=jnp.float32)
        return dict(hidden_states=hidden_states, memory_keys=memory_keys, memory_values=memory_values, attention_mask=attention_mask, Wq=Wq, Wout=Wout, ln_gamma=ln_gamma, ln_beta=ln_beta)
    _L1_xattn_all = _L1_xattn_setup()
    _L1_xattn_in = {k: v for k, v in _L1_xattn_all.items() if k in ('Wq', 'Wout', 'ln_gamma', 'ln_beta')}
    del _L1_xattn_all
    return {'x': x, 'ctx_4096': ctx_4096, 'mask_BxS2_ik0': mask_BxS2_ik0, 'mask_BxS2_bf1': mask_BxS2_bf1, 'L0_xattn_Wq': _L0_xattn_in['Wq'], 'L0_xattn_bq': _L0_xattn_in['bq'], 'L0_xattn_Wk': _L0_xattn_in['Wk'], 'L0_xattn_bk': _L0_xattn_in['bk'], 'L0_xattn_Wv': _L0_xattn_in['Wv'], 'L0_xattn_bv': _L0_xattn_in['bv'], 'L0_xattn_Wo': _L0_xattn_in['Wo'], 'L0_xattn_bo': _L0_xattn_in['bo'], 'L0_xattn_ln_g': _L0_xattn_in['ln_g'], 'L0_xattn_ln_b': _L0_xattn_in['ln_b'], 'L1_xattn_Wq': _L1_xattn_in['Wq'], 'L1_xattn_Wout': _L1_xattn_in['Wout'], 'L1_xattn_ln_gamma': _L1_xattn_in['ln_gamma'], 'L1_xattn_ln_beta': _L1_xattn_in['ln_beta']}

def reference(x, ctx_4096, mask_BxS2_ik0, mask_BxS2_bf1, L0_xattn_Wq, L0_xattn_bq, L0_xattn_Wk, L0_xattn_bk, L0_xattn_Wv, L0_xattn_bv, L0_xattn_Wo, L0_xattn_bo, L0_xattn_ln_g, L0_xattn_ln_b, L1_xattn_Wq, L1_xattn_Wout, L1_xattn_ln_gamma, L1_xattn_ln_beta):
    import jax
    import jax.numpy as jnp

    def _L0_xattn_ref(hidden_states, vision_features, attention_mask, Wq, bq, Wk, bk, Wv, bv, Wo, bo, ln_g, ln_b):
        import jax, jax.numpy as jnp
        import numpy as np
        H = 512
        NH = 32
        HD = H // NH
        B, L, _ = hidden_states.shape
        Vn = vision_features.shape[1]
        Q = (hidden_states @ Wq.T + bq).reshape(B, L, NH, HD)
        K = (vision_features @ Wk.T + bk).reshape(B, Vn, NH, HD)
        Vv = (vision_features @ Wv.T + bv).reshape(B, Vn, NH, HD)
        scores = jnp.einsum('blhd,bvhd->bhlv', Q, K) / np.sqrt(HD).astype(np.float32)
        mask = (attention_mask != 0)[:, None, None, :]
        scores = jnp.where(mask, scores, -jnp.inf)
        attn = jax.nn.softmax(scores, axis=-1)
        ctx = jnp.einsum('bhlv,bvhd->blhd', attn, Vv).reshape(B, L, H)
        attn_out = ctx @ Wo.T + bo
        x = hidden_states + attn_out
        mu = jnp.mean(x, axis=-1, keepdims=True)
        var = jnp.mean(jnp.square(x - mu), axis=-1, keepdims=True)
        return (x - mu) / jnp.sqrt(var + 1e-05) * ln_g + ln_b

    def _L1_xattn_ref(hidden_states, memory_keys, memory_values, attention_mask, Wq, Wout, ln_gamma, ln_beta):
        import jax, jax.numpy as jnp
        import numpy as np
        HIDDEN = 512
        HEADS = 32
        HEAD_DIM = HIDDEN // HEADS
        LN_EPS = 1e-05

        def _split_heads(x):
            B, S, _ = x.shape
            return x.reshape(B, S, HEADS, HEAD_DIM).transpose(0, 2, 1, 3)
        residual = hidden_states
        mu = jnp.mean(hidden_states, axis=-1, keepdims=True)
        var = jnp.var(hidden_states, axis=-1, keepdims=True)
        x = (hidden_states - mu) * jax.lax.rsqrt(var + LN_EPS) * ln_gamma + ln_beta
        Q = _split_heads(x @ Wq.T)
        K = _split_heads(memory_keys)
        V = _split_heads(memory_values)
        scale = HEAD_DIM ** (-0.5)
        scores = jnp.einsum('bhsd,bhtd->bhst', Q, K) * scale
        mask = attention_mask[:, None, None, :]
        scores = jnp.where(mask, scores, -jnp.inf)
        probs = jax.nn.softmax(scores, axis=-1)
        attn = jnp.einsum('bhst,bhtd->bhsd', probs, V)
        B, _, S, _ = attn.shape
        attn = attn.transpose(0, 2, 1, 3).reshape(B, S, HIDDEN)
        out = attn @ Wout.T
        return residual + out
    x = _L0_xattn_ref(x, ctx_4096, mask_BxS2_ik0, L0_xattn_Wq, L0_xattn_bq, L0_xattn_Wk, L0_xattn_bk, L0_xattn_Wv, L0_xattn_bv, L0_xattn_Wo, L0_xattn_bo, L0_xattn_ln_g, L0_xattn_ln_b)
    x = _L1_xattn_ref(x, ctx_4096, ctx_4096, mask_BxS2_bf1, L1_xattn_Wq, L1_xattn_Wout, L1_xattn_ln_gamma, L1_xattn_ln_beta)
    return x

_drawn_inputs = setup_inputs


def setup_inputs(seed=0):
    import zlib

    import numpy as np

    out = dict(_drawn_inputs(seed))
    spreads = {'L0_xattn_bq': (0.0, 0.425),
     'L0_xattn_bk': (0.0, 0.8),
     'L0_xattn_bv': (0.0, 0.1),
     'L0_xattn_bo': (0.0, 0.1),
     'L0_xattn_ln_g': (1.0, 0.2),
     'L0_xattn_ln_b': (0.0, 0.1),
     'L1_xattn_ln_gamma': (1.0, 0.2),
     'L1_xattn_ln_beta': (0.0, 0.304)}
    factors = {}
    for name, (base, spread) in spreads.items():
        noise = np.random.default_rng([zlib.crc32(name.encode()), seed]).standard_normal(out[name].shape)
        drawn = base * np.exp(spread * noise) if base else spread * noise
        out[name] = jnp.asarray(drawn.astype(out[name].dtype))
    for name, factor in factors.items():
        out[name] = (out[name] * factor).astype(out[name].dtype)
    return out
```

```python
from contextlib import ExitStack

import concourse.bass as bass
from concourse import mybir

F32 = mybir.dt.float32
F32R = mybir.dt.float32r
BF16 = mybir.dt.bfloat16
I32 = mybir.dt.int32
U8 = mybir.dt.uint8
ALU = mybir.AluOpType
ACT = mybir.ActivationFunctionType

B, S, T, H = 8, 56, 1500, 512
HD = 16
P = 128
KT = H // P
HU = P // HD
J = 12
TP = T // J
NC = 3
CW = T // NC
JC = J // NC
W = HU * S
PAIRS = 4
PW = 2 * S
CG = 32
UL = KT
U = 2 * UL
RING = 3
EPS = 1e-5
MASKED = -3e38
FLOOR = -1e37
SCALE = HD ** -0.5
VB = H // 32

K_AT = {0: 0, 2: 1, 4: 2}
MAX_AT = {6: 0, 7: 1, 8: 2, 9: 3}
SUM_AT = 3
V_BEFORE_OUT = 3


class Banks:

    def __init__(self):
        k = lambda ct: [("K", ct, c, "dve") for c in range(NC)]
        total = lambda u: [("sum", u, 0, "dve")]
        v = [("V", j, 0, "act" if j % 2 == 0 else "dve") for j in range(J)]
        self.first = [("Q", ct, 0, "act") for ct in range(KT)]
        self.pro = self.first + v + k(0)
        chain = [("out", 0, 0, "dve"), ("z", 0, 0, "dve"), ("Q1", 0, 0, "dve")]
        mixed = lambda ct, u: k(ct)[:2] + total(u) + k(ct)[2:]
        body = k(1) + mixed(2, 0) + mixed(3, 1) + total(2) + total(3) + chain
        body += [x for u in range(UL, U) for x in total(u)]
        out1 = [("out", 1, 0, "dve")]
        self.loop = body + v[:V_BEFORE_OUT] + out1 + v[V_BEFORE_OUT:] + k(0)
        self.tail = body + out1

    def jobs(self, i, last):
        return self.pro if i is None else self.tail if last else self.loop

    def slot(self, i, last, key):
        at = [x[:3] for x in self.jobs(i, last)].index(key)
        base = 0 if i is None else len(self.pro)
        assert len(self.loop) % 2 == 0
        return (base + at) % 2

    def done(self, i, last, key):
        at = [x[:3] for x in self.jobs(i, last)].index(key) + 1
        return at if i is None else i * len(self.loop) + (len(self.pro) + at)

    def freed(self, i, last, key):
        count = lambda js: sum(x[3] == "dve" for x in js)
        jobs = self.jobs(i, last)
        at = [x[:3] for x in jobs].index(key)
        assert jobs[at][3] == "dve"
        here = count(jobs[: at + 1])
        return here if i is None else i * count(self.loop) + (count(self.pro) + here)

    def freed_ahead(self, i):
        count = lambda js: sum(x[3] == "dve" for x in js)
        return i * count(self.loop) + count(self.pro)

    def before(self, i, last, key):
        jobs = self.jobs(i, last)
        at = [x[:3] for x in jobs].index(key) - 2
        count = lambda js, who: sum(x[3] == who for x in js)
        if i is None:
            if at < 0:
                return None
            who = jobs[at][3]
            return who, count(jobs[: at + 1], who)
        if at >= 0:
            who = jobs[at][3]
            return who, i * count(self.loop, who) + (count(self.pro, who) + count(jobs[: at + 1], who))
        assert [x[:3] for x in self.pro[-2:]] == [x[:3] for x in self.loop[-2:]]
        who = self.loop[at][3]
        return who, i * count(self.loop, who) + (count(self.pro, who) - count(self.loop[at:], who) + 1)


class Steps:

    def __init__(self, eng, sem, base, i, per):
        self.eng, self.sem, self.n, self.i, self.per = eng, sem, base, i, per

    def value(self):
        return self.n if self.i is None else self.i * self.per + self.n

    def inc(self, ins):
        self.n += 1
        ins.then_inc(self.sem, 1)

    def wait(self):
        self.eng.wait_ge(self.sem, self.value())


def cross_attention(nc, x, xT, ctx, ctxT, mask0, mask1, mask0T, mask1T,
                    Wq0T, bq, Wk0T, bk, Wv0T, bv, Wo0T, bo, ln_g, ln_b,
                    Wq1T, Wo1T, gamma, beta, ident, headmask, halves, quarters, out):
    banks = Banks()
    stack = ExitStack()
    with stack:
        def sb(name, shape, dt=F32):
            return stack.enter_context(nc.sbuf_tensor(name, shape, dt))

        def psum(name, shape, dt=F32):
            return stack.enter_context(nc.psum_tensor(name, shape, dt))

        def sem(name):
            return stack.enter_context(nc.semaphore(name))

        vals = sb("vals", [P, 2 * J * VB + 1, 32])
        ONES = 2 * J * VB
        e_flat = vals[:, 0:J * VB, :].rearrange("p n c -> p (n c)")
        e_raw = e_flat[:, 0:KT * T].rearrange("p (k t) -> p k t", k=KT)
        a_flat = vals[:, J * VB:2 * J * VB, :].rearrange("p n c -> p (n c)")
        xt_hi = sb("xt_hi", [P, KT, T], F32R)
        xt_lo = sb("xt_lo", [P, KT, T], F32R)
        key_hi = sb("key_hi", [P, 2, T], F32R)
        key_lo = sb("key_lo", [P, 2, T], F32R)
        wk_hi = sb("wk_hi", [P, KT, H], F32R)
        wk_lo = sb("wk_lo", [P, KT, H], F32R)
        wv_hi = sb("wv_hi", [P, KT, H], F32R)
        wv_lo = sb("wv_lo", [P, KT, H], F32R)
        wq1 = sb("wq1", [P, KT, H])
        wo = sb("wo", [P, KT, H])
        q0_all = sb("q0_all", [P, KT, B * S])
        q_hi = sb("q_hi", [P, KT, S], F32R)
        q_lo = sb("q_lo", [P, KT, S])
        blk_hi = sb("blk_hi", [P, 2, HU, S], F32R)
        blk_lo = sb("blk_lo", [P, 2, HU, S], F32R)
        shift = sb("shift", [PW, 2, W], F32R)
        chunk_max = sb("chunk_max", [PW, 2, PAIRS, NC])
        minus_max = sb("minus_max", [PW, 2, PAIRS])
        bias_row = sb("bias_row", [PW, T], BF16)
        bias_col = sb("bias_col", [TP, 2, B, J])
        bias_now = sb("bias_now", [TP, 2, J])
        probs = sb("probs", [P, RING * W])
        norm = probs[0:S, 0:H]
        resid = sb("resid", [S, H])
        g_row = sb("g_row", [S, H])
        b_row = sb("b_row", [S, H])
        bo_row = sb("bo_row", [S, H])
        sums = sb("sums", [P, W])
        numer = sb("numer", [P, PW])
        recip = sb("recip", [P, PW])
        half0 = numer[:, 0:S]
        attn = sb("attn", [P, KT, S])
        zT = sums[:, 0:KT * S].rearrange("p (k s) -> p k s", k=KT)
        cols = sb("cols", [P, 5, KT])
        bq_raw = sb("bq_raw", [P, KT])
        stats = sb("stats", [S, 6])
        mv = sb("mv", [S, 2, 2])
        rstd = sb("rstd", [S, 2, 1])
        vpe = sb("vpe", [S, 2, 1])
        minus_half = sb("minus_half", [S, 1])
        ident_sb = sb("ident_sb", [PW, PW])
        ones_r = sb("ones_r", [PW, TP], F32R)
        quarter = sb("quarter", [P, CG])
        hmask = sb("hmask", [P, HU])
        hsel = sb("hsel", [P, 2])

        sc_ps = [psum(f"sc_ps{n}", [P, 512]) for n in range(2)]
        max_ps = [psum(f"max_ps{n}", [P, 512]) for n in range(2)]
        pv_ps = psum("pv_ps", [P, 512])
        sum_ps = psum("sum_ps", [P, 512])
        job_ps = [psum(f"job_ps{n}", [P, 512]) for n in range(2)]

        bias_dram = nc.dram_tensor("bias_rows", [2, B * J, TP], BF16, kind="Internal").ap()

        s_consts = sem("s_consts")
        s_weights = sem("s_weights")
        s_xT = sem("s_xT")
        s_wo = sem("s_wo")
        s_raw = sem("s_raw")
        s_ctx = sem("s_ctx")
        s_x = sem("s_x")
        s_maskin = sem("s_maskin")
        s_biasout = sem("s_biasout")
        s_bias = sem("s_bias")
        s_out = sem("s_out")
        s_fill = sem("s_fill")
        s_w_hi = sem("s_w_hi")
        s_w_lo = sem("s_w_lo")
        s_bq = sem("s_bq")
        s_mask = sem("s_mask")
        s_job = sem("s_job")
        s_free_act = sem("s_free_act")
        s_free_dve = sem("s_free_dve")
        s_key_hi = sem("s_key_hi")
        s_xt_hi = sem("s_xt_hi")
        s_xt_lo = sem("s_xt_lo")
        s_q = sem("s_q")
        s_blk = sem("s_blk")
        s_max = sem("s_max")
        s_red = sem("s_red")
        s_rowmax = sem("s_rowmax")
        s_shift = sem("s_shift")
        s_score = sem("s_score")
        s_exp = sem("s_exp")
        s_pv = sem("s_pv")
        s_sums = sem("s_sums")
        s_attn = sem("s_attn")
        s_dve = sem("s_dve")
        s_bnow = sem("s_bnow")
        s_passed = sem("s_passed")
        s_resid = sem("s_resid")
        s_var = sem("s_var")
        s_rstd = sem("s_rstd")
        s_norm = sem("s_norm")
        s_zT = sem("s_zT")

        N_SC = U * J
        N_RED = U * PAIRS * NC
        L_RED = UL * PAIRS * NC
        DVE_STEPS = U * 2 + 7
        CONSTS = 13 * 16

        xT_sb = wo[:, :, :].rearrange("p k n -> p (k n)")[:, 0:KT * B * S].rearrange("p (k n) -> p k n", k=KT)
        m0 = B * J
        mask_cols = [probs[0:TP, 0:m0].bitcast(I32), probs[0:TP, 240:240 + m0 // 4].bitcast(U8)]
        mask_rows = [probs[0:m0, 100:100 + TP].bitcast(I32), probs[0:m0, 280:280 + 32].bitcast(U8)[:, 0:TP]]
        bias_bf = probs[0:m0, 600:600 + TP].bitcast(BF16).rearrange("p (l t) -> p l t", l=2)
        L0_KEYS = UL * NC

        block = stack.enter_context(nc.Block())


        def par(u):
            return u % 2

        @block.sync
        def _(sp):
            for src, dst in ((mask0, mask_cols[0]), (mask1, mask_cols[1]), (mask0T, mask_rows[0]), (mask1T, mask_rows[1])):
                sp.dma_start(dst, src).then_inc(s_maskin, 16)
            for dst, src in ((a_flat[:, 0:2048], Wk0T), (a_flat[:, 2048:4096], Wv0T), (a_flat[:, 4096:6144], Wq0T)):
                sp.dma_start(dst.rearrange("p (k n) -> p k n", k=KT), src.rearrange("(k p) n -> p k n", p=P)).then_inc(s_weights, 16)
            sp.dma_start(xT_sb, xT.rearrange("(k p) n -> p k n", p=P)).then_inc(s_xT, 16)
            sp.dma_start(e_raw, ctxT[0].rearrange("(k p) t -> p k t", p=P)).then_inc(s_raw, 16)
            smalls = ((bq_raw[:, :], bq), (cols[:, 1, :], bk), (cols[:, 2, :], bv), (cols[:, 3, :], gamma),
                      (cols[:, 4, :], beta), (ident_sb[:, :], ident),
                      (hmask[:, :], headmask), (hsel[:, :], halves), (quarter[:, :], quarters))
            for dst, src in smalls:
                sp.dma_start(dst, src).then_inc(s_consts, 16)
            for dst, src in ((g_row, ln_g), (b_row, ln_b), (bo_row, bo)):
                sp.dma_start(dst[:, :], src.partition_broadcast(S)).then_inc(s_consts, 16)
            sp.dma_start(wq1[:, :, :], Wq1T.rearrange("(k p) n -> p k n", p=P)).then_inc(s_consts, 16)
            sp.wait_ge(s_mask, 4)
            for layer in range(2):
                sp.dma_start(bias_dram[layer], bias_bf[:, layer, :]).then_inc(s_biasout, 16)
            sp.wait_ge(s_biasout, 32)
            sp.dma_start(bias_row[:, :], bias_dram[0, 0:J, :].rearrange("j p -> (j p)").partition_broadcast(PW)).then_inc(s_bias, 16)
            sp.wait_ge(s_job, banks.done(None, False, ("Q", KT - 1, 0)))
            sp.dma_start(wo[:, :, :], Wo0T.rearrange("(k p) n -> p k n", p=P)).then_inc(s_wo, 16)
            sp.dma_start(resid[:, :], x[0]).then_inc(s_x, 16)
            sp.wait_ge(s_w_lo, 2)
            sp.dma_start(a_flat[0:TP, :], ctx[0].rearrange("(p j) d -> p (j d)", j=J)).then_inc(s_ctx, 16)

            def batch(i, last):
                sp.wait_ge(s_red, i * N_RED + L_RED)
                sp.dma_start(bias_row[:, :], bias_dram[1, bass.ts(i, J), :].rearrange("j p -> (j p)").partition_broadcast(PW)).then_inc(s_bias, 16)
                if not last:
                    sp.wait_ge(s_pv, i * N_SC + UL * J)
                    sp.dma_start(e_raw, ctxT[i + 1].rearrange("(k p) t -> p k t", p=P)).then_inc(s_raw, 16)
                sp.wait_ge(s_job, banks.done(i, last, ("out", 0, 0)))
                sp.dma_start(wo[:, :, :], Wo1T.rearrange("(k p) n -> p k n", p=P)).then_inc(s_wo, 16)
                if not last:
                    sp.wait_ge(s_red, i * N_RED + N_RED)
                    sp.dma_start(bias_row[:, :], bias_dram[0, bass.ts(i + 1, J), :].rearrange("j p -> (j p)").partition_broadcast(PW)).then_inc(s_bias, 16)
                    sp.wait_ge(s_pv, (i + 1) * N_SC)
                    sp.dma_start(a_flat[0:TP, :], ctx[i + 1].rearrange("(p j) d -> p (j d)", j=J)).then_inc(s_ctx, 16)
                sp.wait_ge(s_free_dve, banks.freed(i, last, ("out", 1, 0)))
                sp.dma_start(out[i], resid[:, :]).then_inc(s_out, 16)
                if not last:
                    sp.dma_start(wo[:, :, :], Wo0T.rearrange("(k p) n -> p k n", p=P)).then_inc(s_wo, 16)
                    sp.wait_ge(s_out, i * 16 + 16)
                    sp.dma_start(resid[:, :], x[i + 1]).then_inc(s_x, 16)

            with sp.Fori(0, B - 1) as i:
                batch(i, False)
            batch(B - 1, True)
            sp.wait_ge(s_out, B * 16)

        @block.tensor
        def _(pe):
            def take_bank(i, last, key):
                if (need := banks.before(i, last, key)) is not None:
                    pe.wait_ge(s_free_act if need[0] == "act" else s_free_dve, need[1])
                return job_ps[banks.slot(i, last, key)]

            def split_product(dst, terms, more=False):
                for n, (a, b) in enumerate(terms):
                    mm = pe.matmul(dst, a, b, start=n == 0, stop=n == len(terms) - 1 and not more)
                return mm

            def project_key(i, last, ct, c):
                bank = take_bank(i, last, ("K", ct, c))
                w = slice(ct * P, (ct + 1) * P)
                t = slice(c * CW, (c + 1) * CW)
                terms = []
                for k in range(KT):
                    terms += [(wk_hi[:, k, w], xt_hi[:, k, t]), (wk_hi[:, k, w], xt_lo[:, k, t]), (wk_lo[:, k, w], xt_hi[:, k, t])]
                split_product(bank[:, 0:CW], terms).then_inc(s_job, 1)

            def project_value(i, last, j):
                bank = take_bank(i, last, ("V", j, 0))
                t = slice(j * TP, (j + 1) * TP)
                terms = []
                for k in range(KT):
                    terms += [(xt_hi[:, k, t], wv_hi[:, k, :]), (xt_hi[:, k, t], wv_lo[:, k, :]), (xt_lo[:, k, t], wv_hi[:, k, :])]
                split_product(bank[0:TP, :], terms).then_inc(s_job, 1)

            def max_rows(i, u, p):
                if p == 0:
                    pe.wait_ge(s_blk, (i * U + (u + 1)) * 2)
                    if u % U < UL:
                        pe.wait_ge(s_key_hi, (i * L0_KEYS + ((u // U) * L0_KEYS + (u % U + 1) * NC)))
                keys = key_hi[:, par(u), :] if u % U < UL else xt_hi[:, u % U - UL, :]
                q = blk_hi[:, par(u), 2 * p:2 * p + 2, :].rearrange("p h s -> p (h s)")
                for c in range(NC):
                    n = (u * PAIRS + p) * NC + c
                    if not (isinstance(i, int) and i == 0 and n < 2):
                        pe.wait_ge(s_red, i * N_RED + (n - 1))
                    pe.matmul(max_ps[n % 2][0:PW, 0:CW], q, keys[:, c * CW:(c + 1) * CW], start=True, stop=True).then_inc(s_max, 1)

            def score(i, last, u, j):
                n = u * J + j
                if n >= 2:
                    pe.wait_ge(s_exp, i * N_SC + (n - 1))
                if j == 0:
                    pe.wait_ge(s_shift, i * U + (u + 1))
                    if u < UL:
                        pe.wait_ge(s_free_dve, banks.freed(i, last, ("K", u, NC - 1)) if u else banks.freed_ahead(i))
                t = slice(j * TP, (j + 1) * TP)
                if u < UL:
                    hi, lo = key_hi[:, par(u), t], key_lo[:, par(u), t]
                else:
                    hi, lo = xt_hi[:, u - UL, t], xt_lo[:, u - UL, t]
                qh = blk_hi[:, par(u), :, :].rearrange("p h s -> p (h s)")
                ql = blk_lo[:, par(u), :, :].rearrange("p h s -> p (h s)")
                terms = [(hi, qh), (hi, ql), (lo, qh), (ones_r[:, :], shift[:, par(u), :])]
                split_product(sc_ps[n % 2][0:TP, 0:W], terms).then_inc(s_score, 1)

            def weigh(i, u, j):
                n = u * J + j
                pe.wait_ge(s_exp, i * N_SC + (n + 1))
                if j == 0:
                    if u:
                        pe.wait_ge(s_sums, (i * U + u) * 2)
                    if u == UL:
                        pe.wait_ge(s_ctx, i * 16 + 16)
                ring = (n % RING) * W
                for p in range(PAIRS):
                    v0 = (u % UL) * PAIRS + p + (0 if u < UL else J * VB) + j * VB
                    pe.matmul(pv_ps[CG * p:CG * p + CG, 0:PW], vals[0:TP, v0, :], probs[0:TP, ring + p * PW:ring + (p + 1) * PW],
                              start=j == 0, stop=j == J - 1, skip_group_check=True, tile_position=(0, CG * p))
                q0 = CG * (j % 4)
                pe.matmul(sum_ps[q0:q0 + CG, 0:W], vals[0:TP, ONES, :], probs[0:TP, ring:ring + W],
                          start=j < 4, stop=j >= J - 4, skip_group_check=True, tile_position=(0, q0)).then_inc(s_pv, 1)

            def total(i, last, u):
                bank = take_bank(i, last, ("sum", u, 0))
                pe.wait_ge(s_sums, (i * U + (u + 1)) * 2)
                for p in range(PAIRS):
                    mm = pe.matmul(bank[CG * p:CG * p + CG, 0:PW], quarter[:, :], sums[:, p * PW:(p + 1) * PW],
                                   start=True, stop=True, tile_position=(0, CG * p))
                mm.then_inc(s_job, 1)

            def output(i, last, layer):
                bank = take_bank(i, last, ("out", layer, 0))
                pe.wait_ge(s_attn, i * U + (layer + 1) * UL)
                pe.wait_ge(s_wo, i * 32 + 16 * (layer + 1))
                for k in range(KT):
                    mm = pe.matmul(bank[0:S, :], attn[:, k, :], wo[:, k, :], start=k == 0, stop=k == KT - 1)
                mm.then_inc(s_job, 1)

            def main_pass(i, last, u):
                for j in range(J):
                    score(i, last, u, j)
                    if (u % UL, j) != (0, 0):
                        weigh(i, u - (j == 0), (j - 1) % J)
                    if u % UL != UL - 1:
                        if j in K_AT and u < UL:
                            project_key(i, last, u + 1, K_AT[j])
                        if j in MAX_AT:
                            max_rows(i, u + 1, MAX_AT[j])
                    if j == SUM_AT and u % UL:
                        total(i, last, u - 1)
                if u % UL == UL - 1:
                    weigh(i, u, J - 1)
                    total(i, last, u)

            pe.wait_ge(s_weights, 48)
            pe.wait_ge(s_xT, 16)
            wq0 = a_flat[:, 4096:6144].rearrange("p (k n) -> p k n", k=KT)
            for ct in range(KT):
                bank = take_bank(None, False, ("Q", ct, 0))
                for k in range(KT):
                    mm = pe.matmul(bank[:, 0:B * S], wq0[:, k, ct * P:(ct + 1) * P], xT_sb[:, k, :], start=k == 0, stop=k == KT - 1)
                mm.then_inc(s_job, 1)
            pe.wait_ge(s_w_hi, 2)
            pe.wait_ge(s_w_lo, 2)
            pe.wait_ge(s_xt_lo, KT)
            for j in range(J):
                project_value(None, False, j)
            for c in range(NC):
                project_key(None, False, 0, c)
            pe.wait_ge(s_fill, 3)
            for p in range(PAIRS):
                max_rows(0, 0, p)

            def batch(i, last):
                for u in range(UL):
                    main_pass(i, last, u)
                output(i, last, 0)
                pe.wait_ge(s_consts, CONSTS)
                bank = take_bank(i, last, ("z", 0, 0))
                pe.wait_ge(s_norm, i + 1)
                pe.sem_inc(s_passed, 1)
                for k in range(KT):
                    mm = pe.transpose(bank[:, k * S:(k + 1) * S], norm[:, k * P:(k + 1) * P], ident_sb[0:S, 0:S])
                mm.then_inc(s_job, 1)
                bank = take_bank(i, last, ("Q1", 0, 0))
                pe.wait_ge(s_zT, i + 1)
                for ct in range(KT):
                    for k in range(KT):
                        mm = pe.matmul(bank[:, ct * S:(ct + 1) * S], wq1[:, k, ct * P:(ct + 1) * P], zT[:, k, :],
                                       start=k == 0, stop=k == KT - 1)
                mm.then_inc(s_job, 1)
                for p in range(PAIRS):
                    max_rows(i, UL, p)
                for u in range(UL, U):
                    main_pass(i, last, u)
                if last:
                    output(i, last, 1)
                    return
                pe.wait_ge(s_xt_lo, i * KT + 2 * KT)
                for j in range(J):
                    if j == V_BEFORE_OUT:
                        output(i, last, 1)
                    project_value(i, last, j)
                for c in range(NC):
                    project_key(i, last, 0, c)
                for p in range(PAIRS):
                    max_rows(i, U, p)

            with pe.Fori(0, B - 1) as i:
                batch(i, False)
            batch(B - 1, True)

        @block.scalar
        def _(act):
            def key_hi_part(i, last, ct, c):
                act.wait_ge(s_job, banks.done(i, last, ("K", ct, c)))
                nc.scalar.activation(key_hi[:, par(ct), c * CW:(c + 1) * CW], job_ps[banks.slot(i, last, ("K", ct, c))][:, 0:CW],
                                     ACT.Identity, bias=cols[:, 1, ct:ct + 1]).then_inc(s_key_hi, 1)

            def value_tile(i, last, j):
                act.wait_ge(s_job, banks.done(i, last, ("V", j, 0)))
                nc.scalar.activation(e_flat[0:TP, j * H:(j + 1) * H], job_ps[banks.slot(i, last, ("V", j, 0))][0:TP, :],
                                     ACT.Copy).then_inc(s_free_act, 1)

            def copy_sums(i, last, u):
                act.wait_ge(s_pv, i * N_SC + (u + 1) * J)
                act.wait_ge(s_job, banks.done(i, last, ("sum", u - 1, 0)) if u else i * len(banks.loop) + len(banks.pro))
                if u:
                    act.wait_ge(s_attn, i * U + u)
                else:
                    act.wait_ge(s_free_dve, banks.freed_ahead(i))
                nc.scalar.activation(numer[:, :], pv_ps[:, 0:PW], ACT.Copy).then_inc(s_sums, 1)
                nc.scalar.activation(sums[:, :], sum_ps[:, 0:W], ACT.Copy).then_inc(s_sums, 1)

            act.wait_ge(s_bq, 1)
            act.wait_ge(s_consts, CONSTS)
            for ct in range(KT):
                act.wait_ge(s_job, banks.done(None, False, ("Q", ct, 0)))
                nc.scalar.activation(q0_all[:, ct, :], job_ps[banks.slot(None, False, ("Q", ct, 0))][:, 0:B * S], ACT.Identity,
                                     bias=cols[:, 0, ct:ct + 1], scale=SCALE).then_inc(s_free_act, 1)
            for j in range(0, J, 2):
                value_tile(None, False, j)
            for c in range(NC):
                key_hi_part(None, False, 0, c)

            def batch(i, last):
                for u in range(U):
                    layer = u // UL
                    if u % UL == 0:
                        act.wait_ge(s_bnow, i * 2 + (layer + 1))
                    for j in range(J):
                        if j == 1 and u % UL:
                            copy_sums(i, last, u - 1)
                        n = u * J + j
                        act.wait_ge(s_score, i * N_SC + (n + 1))
                        if n >= RING:
                            act.wait_ge(s_pv, i * N_SC + (n + 1 - RING))
                        if u == UL and j == 0:
                            act.wait_ge(s_job, banks.done(i, last, ("z", 0, 0)))
                        nc.scalar.activation(probs[0:TP, (n % RING) * W:(n % RING + 1) * W], sc_ps[n % 2][0:TP, 0:W],
                                             ACT.Exp, bias=bias_now[:, layer, j:j + 1]).then_inc(s_exp, 1)
                        if j in K_AT and u < UL - 1:
                            key_hi_part(i, last, u + 1, K_AT[j])
                    if u % UL == UL - 1:
                        copy_sums(i, last, u)
                if last:
                    return
                for j in range(0, J, 2):
                    value_tile(i, last, j)
                for c in range(NC):
                    key_hi_part(i, last, 0, c)

            with act.Fori(0, B - 1) as i:
                batch(i, False)
            batch(B - 1, True)

        @block.vector
        def _(dve):
            def key_lo_part(i, last, ct, c):
                t = slice(c * CW, (c + 1) * CW)
                dve.wait_ge(s_key_hi, ct * NC + c + 1 if i is None else i * L0_KEYS + ((ct == 0) * L0_KEYS + ct * NC + c + 1))
                nc.vector.scalar_tensor_tensor(out=key_lo[:, par(ct), t], in0=job_ps[banks.slot(i, last, ("K", ct, c))][:, 0:CW],
                                               scalar=cols[:, 1, ct:ct + 1], in1=key_hi[:, par(ct), t].bitcast(F32),
                                               op0=ALU.add, op1=ALU.subtract).then_inc(s_free_dve, 1)

            def value_tile(i, last, j):
                dve.wait_ge(s_job, banks.done(i, last, ("V", j, 0)))
                nc.vector.tensor_copy(e_flat[0:TP, j * H:(j + 1) * H], job_ps[banks.slot(i, last, ("V", j, 0))][0:TP, :]).then_inc(s_free_dve, 1)

            def take_max(i, u, p):
                if p == 0:
                    if not (isinstance(i, int) and i == 0 and u == 0):
                        dve.wait_ge(s_shift, i * U + u)
                    dve.wait_ge(s_bias, i * 32 + 16 * (1 + u // UL))
                for c in range(NC):
                    n = (u * PAIRS + p) * NC + c
                    dve.wait_ge(s_max, i * N_RED + (n + 1))
                    dve.sem_inc(s_passed, 1)
                    at = max_ps[n % 2][0:PW, 0:CW]
                    nc.vector.tensor_tensor_reduce(out=at, in0=at, in1=bias_row[:, c * CW:(c + 1) * CW], scale=1.0, scalar=FLOOR,
                                                   op0=ALU.add, op1=ALU.max, accum_out=chunk_max[:, par(u), p, c:c + 1]).then_inc(s_red, 1)
                if p == PAIRS - 1:
                    dve.wait_ge(s_red, i * N_RED + (n + 1))
                    nc.vector.tensor_reduce(minus_max[:, par(u), :], chunk_max[:, par(u), :, :], mybir.AxisListType.X, ALU.max, negate=True).then_inc(s_rowmax, 1)

            def divide(i, last, u, step):
                dve.wait_ge(s_job, banks.done(i, last, ("sum", u, 0)))
                nc.vector.reciprocal(recip[:, :], job_ps[banks.slot(i, last, ("sum", u, 0))][:, 0:PW]).then_inc(s_free_dve, 1)
                dve.wait_ge(s_free_dve, banks.freed(i, last, ("sum", u, 0)))
                step.inc(nc.vector.tensor_tensor(recip[:, :], numer[:, :], recip[:, :], ALU.mult))
                step.wait()
                ct = u % UL
                step.inc(nc.vector.tensor_scalar(half0[:, :], recip[:, 0:S], hsel[:, 0:1], cols[:, 2, ct:ct + 1] if u < UL else 0.0,
                                                 ALU.mult, ALU.add))
                step.wait()
                nc.vector.scalar_tensor_tensor(out=attn[:, ct, :], in0=recip[:, S:2 * S], scalar=hsel[:, 1:2], in1=half0[:, :],
                                               op0=ALU.mult, op1=ALU.add).then_inc(s_attn, 1)

            def layer_norm(i, n, src, dst, step):
                step.inc(nc.vector.bn_stats(stats[:, :], src))
                step.wait()
                dve.sem_inc(s_passed, 1)
                step.inc(nc.vector.bn_aggr(mv[:, n, :], stats[:, :]))
                step.wait()
                nc.vector.tensor_scalar(vpe[:, n, :], mv[:, n, 1:2], EPS, None, ALU.add).then_inc(s_var, 1)
                dve.wait_ge(s_rstd, i * 2 + (n + 1))
                return nc.vector.tensor_scalar(dst, src, mv[:, n, 0:1], rstd[:, n, :], ALU.subtract, ALU.mult)

            nc.vector.memset(vals[:, ONES, :], 1.0).then_inc(s_fill, 1)
            nc.vector.memset(ones_r[:, :].bitcast(F32), 1.0).then_inc(s_fill, 1)
            nc.vector.memset(minus_half[:, :], -0.5).then_inc(s_fill, 1)
            dve.wait_ge(s_maskin, 64)
            for layer in range(2):
                nc.vector.tensor_scalar(bias_col[:, layer, :, :].rearrange("p b j -> p (b j)"), mask_cols[layer], 0.0, MASKED, ALU.is_equal, ALU.mult).then_inc(s_mask, 1)
                nc.vector.tensor_scalar(bias_bf[:, layer, :], mask_rows[layer], 0.0, MASKED, ALU.is_equal, ALU.mult).then_inc(s_mask, 1)
            dve.wait_ge(s_mask, 4)
            nc.vector.tensor_copy(bias_now[:, 0, :], bias_col[:, 0, 0, :]).then_inc(s_bnow, 1)
            dve.wait_ge(s_consts, CONSTS)
            nc.vector.tensor_scalar(cols[:, 0, :], bq_raw[:, :], SCALE, None, ALU.mult).then_inc(s_bq, 1)
            dve.wait_ge(s_weights, 48)
            for n, (hi, lo) in enumerate(((wk_hi, wk_lo), (wv_hi, wv_lo))):
                raw = a_flat[:, n * 2048:(n + 1) * 2048].rearrange("p (k n) -> p k n", k=KT)
                nc.vector.tensor_copy(hi[:, :, :], raw).then_inc(s_w_hi, 1)
                dve.wait_ge(s_w_hi, n + 1)
                nc.vector.tensor_tensor(lo[:, :, :], raw, hi[:, :, :].bitcast(F32), ALU.subtract).then_inc(s_w_lo, 1)
            for j in range(1, J, 2):
                value_tile(None, False, j)
            dve.wait_ge(s_free_act, KT)

            def queries0(b, count):
                q = q0_all[:, :, bass.ts(b, S)]
                nc.vector.tensor_copy(q_hi[:, :, :], q).then_inc(s_q, 1)
                dve.wait_ge(s_q, count + 1)
                nc.vector.tensor_tensor(q_lo[:, :, :], q, q_hi[:, :, :].bitcast(F32), ALU.subtract).then_inc(s_q, 1)

            queries0(0, 0)
            for c in range(NC):
                key_lo_part(None, False, 0, c)
            for p in range(PAIRS):
                take_max(0, 0, p)

            def batch(i, last):
                step = Steps(dve, s_dve, 0, i, DVE_STEPS)
                for u in range(U):
                    for j in range(J):
                        if j == SUM_AT and u % UL:
                            divide(i, last, u - 1, step)
                        if u % UL != UL - 1:
                            if j in K_AT and u < UL:
                                key_lo_part(i, last, u + 1, K_AT[j])
                            if j in MAX_AT:
                                take_max(i, u + 1, MAX_AT[j])
                    if u == 1:
                        nc.vector.tensor_copy(bias_now[:, 1, :], bias_col[:, 1, bass.ds(i, 1), :].rearrange("p b j -> p (b j)")).then_inc(s_bnow, 1)
                    if u == UL + 1 and not last:
                        dve.wait_ge(s_exp, i * N_SC + UL * J)
                        nc.vector.tensor_copy(bias_now[:, 0, :], bias_col[:, 0, bass.ds(i + 1, 1), :].rearrange("p b j -> p (b j)")).then_inc(s_bnow, 1)
                    if u == UL - 1:
                        divide(i, last, u, step)
                        dve.wait_ge(s_resid, i + 1)
                        dve.wait_ge(s_job, banks.done(i, last, ("out", 0, 0)))
                        nc.vector.tensor_tensor(resid[:, :], job_ps[banks.slot(i, last, ("out", 0, 0))][0:S, :], resid[:, :], ALU.add).then_inc(s_free_dve, 1)
                        dve.wait_ge(s_free_dve, banks.freed(i, last, ("out", 0, 0)))
                        step.inc(layer_norm(i, 0, resid[:, :], resid[:, :], step))
                        step.wait()
                        step.inc(nc.vector.tensor_tensor(resid[:, :], resid[:, :], g_row[:, :], ALU.mult))
                        step.wait()
                        step.inc(nc.vector.tensor_tensor(resid[:, :], resid[:, :], b_row[:, :], ALU.add))
                        step.wait()
                        layer_norm(i, 1, resid[:, :], norm, step).then_inc(s_norm, 1)
                        dve.wait_ge(s_job, banks.done(i, last, ("z", 0, 0)))
                        bank = job_ps[banks.slot(i, last, ("z", 0, 0))][:, 0:KT * S].rearrange("p (k s) -> p k s", k=KT)
                        nc.vector.tensor_tensor(zT[:, :, :], bank, cols[:, 3, :].unsqueeze(2).to_broadcast([P, KT, S]), ALU.mult).then_inc(s_free_dve, 1)
                        dve.wait_ge(s_free_dve, banks.freed(i, last, ("z", 0, 0)))
                        nc.vector.tensor_tensor(zT[:, :, :], zT[:, :, :], cols[:, 4, :].unsqueeze(2).to_broadcast([P, KT, S]), ALU.add).then_inc(s_zT, 1)
                        dve.wait_ge(s_blk, i * U * 2 + UL * 2)
                        dve.wait_ge(s_job, banks.done(i, last, ("Q1", 0, 0)))
                        bank = job_ps[banks.slot(i, last, ("Q1", 0, 0))][:, 0:KT * S].rearrange("p (k s) -> p k s", k=KT)
                        nc.vector.tensor_scalar(q_hi[:, :, :], bank, SCALE, None, ALU.mult).then_inc(s_q, 1)
                        dve.wait_ge(s_q, i * 3 + 3)
                        nc.vector.scalar_tensor_tensor(out=q_lo[:, :, :], in0=bank, scalar=SCALE, in1=q_hi[:, :, :].bitcast(F32),
                                                       op0=ALU.mult, op1=ALU.subtract).then_inc(s_free_dve, 1)
                        for p in range(PAIRS):
                            take_max(i, UL, p)
                divide(i, last, U - 1, step)

                def finish():
                    dve.wait_ge(s_job, banks.done(i, last, ("out", 1, 0)))
                    nc.vector.tensor_tensor(resid[:, :], job_ps[banks.slot(i, last, ("out", 1, 0))][0:S, :], resid[:, :], ALU.add).then_inc(s_free_dve, 1)

                if last:
                    finish()
                else:
                    dve.wait_ge(s_blk, i * U * 2 + U * 2)
                    queries0(i + 1, i * 3 + 3)
                    for j in range(J):
                        if j == V_BEFORE_OUT:
                            finish()
                        if j % 2:
                            value_tile(i, last, j)
                    for c in range(NC):
                        key_lo_part(i, last, 0, c)
                    for p in range(PAIRS):
                        take_max(i, U, p)
                assert step.n == DVE_STEPS, step.n

            with dve.Fori(0, B - 1) as i:
                batch(i, False)
            batch(B - 1, True)

        @block.gpsimd
        def _(pool):
            def split_context(i, ct):
                nc.gpsimd.tensor_copy(xt_hi[:, ct, :], e_raw[:, ct, :]).then_inc(s_xt_hi, 1)
                pool.wait_ge(s_xt_hi, ct + 1 if i is None else i * KT + (KT + ct + 1))
                nc.gpsimd.tensor_tensor(xt_lo[:, ct, :], e_raw[:, ct, :], xt_hi[:, ct, :].bitcast(F32), ALU.subtract).then_inc(s_xt_lo, 1)

            def spread_queries(i, last, u):
                ct = u % UL
                shape = [P, HU, S]
                m = hmask[:, :].unsqueeze(2).to_broadcast(shape)
                if UL <= u < U:
                    pool.wait_ge(s_free_dve, banks.freed(i, last, ("Q1", 0, 0)))
                else:
                    pool.wait_ge(s_q, i * 3 + (2 if u < UL else 5))
                if u >= 2:
                    pool.wait_ge(s_score, i * N_SC + (u - 1) * J)
                nc.gpsimd.tensor_tensor(blk_hi[:, par(u), :, :], q_hi[:, ct, :].bitcast(F32).unsqueeze(1).to_broadcast(shape), m, ALU.mult).then_inc(s_blk, 1)
                nc.gpsimd.tensor_tensor(blk_lo[:, par(u), :, :], q_lo[:, ct, :].unsqueeze(1).to_broadcast(shape), m, ALU.mult).then_inc(s_blk, 1)

            def spread_max(i, u):
                pool.wait_ge(s_rowmax, i * U + (u + 1))
                shape = [PW, PAIRS, PW]
                nc.gpsimd.tensor_tensor(shift[:, par(u), :].rearrange("p (a c) -> p a c", a=PAIRS),
                                        ident_sb[:, :].unsqueeze(1).to_broadcast(shape),
                                        minus_max[:, par(u), :].unsqueeze(2).to_broadcast(shape), ALU.mult).then_inc(s_shift, 1)

            pool.wait_ge(s_raw, 16)
            for ct in range(KT):
                split_context(None, ct)
            pool.wait_ge(s_consts, CONSTS)
            pool.wait_ge(s_fill, 3)
            spread_queries(0, False, 0)
            spread_max(0, 0)

            def batch(i, last):
                spread_queries(i, last, 1)
                pool.wait_ge(s_x, i * 16 + 16)
                nc.gpsimd.tensor_tensor(resid[:, :], resid[:, :], bo_row[:, :], ALU.add).then_inc(s_resid, 1)
                spread_max(i, 1)
                for u in range(1, UL - 1):
                    spread_queries(i, last, u + 1)
                    spread_max(i, u + 1)
                for n in range(2):
                    pool.wait_ge(s_var, i * 2 + (n + 1))
                    nc.gpsimd.tensor_tensor(rstd[:, n, :], vpe[:, n, :], minus_half[:, :], ALU.pow).then_inc(s_rstd, 1)
                spread_queries(i, last, UL)
                spread_max(i, UL)
                for u in range(UL, U):
                    if u + 1 < U:
                        spread_queries(i, last, u + 1)
                    if not last and u > UL:
                        pool.wait_ge(s_raw, i * 16 + 32)
                        pool.wait_ge(s_score, i * N_SC + u * J)
                        pool.sem_inc(s_passed, 1)
                        split_context(i, u - 1 - UL)
                    if u + 1 < U:
                        spread_max(i, u + 1)
                if not last:
                    pool.wait_ge(s_score, i * N_SC + U * J)
                    pool.sem_inc(s_passed, 1)
                    split_context(i, KT - 1)
                    spread_queries(i, last, U)
                    spread_max(i, U)

            with pool.Fori(0, B - 1) as i:
                batch(i, False)
            batch(B - 1, True)


def kernel(x, ctx_4096, mask_BxS2_ik0, mask_BxS2_bf1, L0_xattn_Wq, L0_xattn_bq, L0_xattn_Wk, L0_xattn_bk,
           L0_xattn_Wv, L0_xattn_bv, L0_xattn_Wo, L0_xattn_bo, L0_xattn_ln_g, L0_xattn_ln_b,
           L1_xattn_Wq, L1_xattn_Wout, L1_xattn_ln_gamma, L1_xattn_ln_beta):
    import numpy as np
    import concourse.bacc as bacc
    from concourse.bass_utils import run_bass_kernel_spmd

    x, ctx = np.asarray(x), np.asarray(ctx_4096)
    mask0 = np.asarray(mask_BxS2_ik0)
    mask1 = np.asarray(mask_BxS2_bf1).view(np.uint8)
    by_channel = lambda v: np.ascontiguousarray(np.asarray(v).reshape(KT, P).T)
    turned = lambda w: np.ascontiguousarray(np.asarray(w).T)
    positions = lambda m: np.ascontiguousarray(m.reshape(B, TP, J).transpose(1, 0, 2).reshape(TP, B * J))
    heads = np.arange(P)[:, None] // HD == np.arange(HU)[None, :]
    halves = (np.arange(P)[:, None] // HD) % 2 == np.arange(2)[None, :]
    arrays = {
        "x": x,
        "xT": turned(x.reshape(B * S, H)),
        "ctx": ctx,
        "ctxT": np.ascontiguousarray(ctx.reshape(B, TP, J, H).transpose(0, 3, 2, 1).reshape(B, H, T)),
        "mask0": positions(mask0), "mask1": positions(mask1),
        "mask0T": turned(positions(mask0)), "mask1T": turned(positions(mask1)),
        "Wq0T": turned(L0_xattn_Wq), "bq": by_channel(L0_xattn_bq),
        "Wk0T": turned(L0_xattn_Wk), "bk": by_channel(L0_xattn_bk),
        "Wv0T": turned(L0_xattn_Wv), "bv": by_channel(L0_xattn_bv),
        "Wo0T": turned(L0_xattn_Wo), "bo": np.asarray(L0_xattn_bo),
        "ln_g": np.asarray(L0_xattn_ln_g), "ln_b": np.asarray(L0_xattn_ln_b),
        "Wq1T": turned(L1_xattn_Wq), "Wo1T": turned(L1_xattn_Wout),
        "gamma": by_channel(L1_xattn_ln_gamma), "beta": by_channel(L1_xattn_ln_beta),
        "ident": np.eye(PW, dtype=np.float32),
        "headmask": heads.astype(np.float32), "halves": halves.astype(np.float32),
        "quarters": np.repeat(np.arange(P)[:, None] % CG == 0, CG, 1).astype(np.float32),
    }
    nc = bacc.Bacc("TRN2", target_bir_lowering=False, num_devices=1)
    args = {n: nc.dram_tensor(f"in_{n}_dram", a.shape, mybir.dt.from_np(a.dtype), kind="ExternalInput").ap() for n, a in arrays.items()}
    args["out"] = nc.dram_tensor("out_dram", (B, S, H), F32, kind="ExternalOutput").ap()
    cross_attention(nc, **args)
    r = run_bass_kernel_spmd(nc, [{f"in_{n}_dram": a for n, a in arrays.items()}], core_ids=[0])
    return r.results[0]["out_dram"]
```

```python
from contextlib import ExitStack

import concourse.bass as bass
from concourse import mybir

F32 = mybir.dt.float32
F32R = mybir.dt.float32r
BF16 = mybir.dt.bfloat16
I32 = mybir.dt.int32
U8 = mybir.dt.uint8
ALU = mybir.AluOpType
ACT = mybir.ActivationFunctionType

B, S, T, H = 8, 56, 1500, 512
HD = 16
P = 128
KT = H // P
HU = P // HD
J = 12
TP = T // J
NC = 3
CW = T // NC
JC = J // NC
W = HU * S
PAIRS = 4
PW = 2 * S
CG = 32
UL = KT
U = 2 * UL
RING = 3
EPS = 1e-5
MASKED = -3e38
FLOOR = -1e37
SCALE = HD ** -0.5
VB = H // 32

K_AT = {0: 0, 1: 1, 2: 2}
MAX_AT = ({1: 2, 2: 2, 3: 2, 4: 2, 5: 1, 6: 1, 7: 1, 8: 1},
          {2: 2, 3: 1, 4: 2, 5: 1, 6: 2, 7: 1, 8: 2, 9: 1})
SUM_AT = 3
SPLIT_OF = {3: 0, 4: 3, 5: 4, 6: 5, 7: 6}
SPLIT_AT = {1: 0, 2: 1, 3: 2, 4: 3}
PARTS = 4
PT = T // PARTS
JV = J // PARTS
BETWEEN_LAYERS = [("V", 0), ("sum", 3), ("V", 1), ("out", 0), ("V", 2), ("V", 3), ("z", 0), ("V", 4), ("Q1", 0),
                  ("V", 5), 2, ("V", 6), 4, ("V", 7), 6, ("V", 8)]
BETWEEN_BATCHES = [("V", 9), ("sum", 7), ("V", 10), ("out", 1), ("K", 0), ("K", 1), 2, ("K", 2), 2, ("V", 11), 8]


class Banks:

    def __init__(self):
        job = lambda kind, n: (kind, n, "act" if kind in ("V", "Q") else "dve")
        key = lambda ct: [job("K", ct * NC + c) for c in range(NC)]
        between = lambda plan: [job(*x) for x in plan if isinstance(x, tuple)]
        self.pro = [job("Q", ct) for ct in range(KT)] + [job("V", j) for j in range(J - 1)] + key(0) + [job("V", J - 1)]
        layer0 = key(1) + key(2) + [job("sum", 0)] + key(3) + [job("sum", 1), job("sum", 2)]
        layer1 = [job("sum", u) for u in range(UL, U - 1)]
        self.loop = layer0 + between(BETWEEN_LAYERS) + layer1 + between(BETWEEN_BATCHES)
        skip = lambda js: [x for x in js if x[0] != "V"]
        self.tail = layer0 + skip(between(BETWEEN_LAYERS)) + layer1 + [job("sum", U - 1), job("out", 1)]
        assert len(self.loop) % 2 == 0 and self.pro[-2:] == self.loop[-2:]

    def jobs(self, i, last):
        return self.pro if i is None else self.tail if last else self.loop

    def slot(self, i, last, key):
        at = [x[:2] for x in self.jobs(i, last)].index(key)
        base = 0 if i is None else len(self.pro)
        assert len(self.loop) % 2 == 0
        return (base + at) % 2

    def done(self, i, last, key):
        at = [x[:2] for x in self.jobs(i, last)].index(key) + 1
        return at if i is None else i * len(self.loop) + (len(self.pro) + at)

    def freed(self, i, last, key):
        count = lambda js: sum(x[2] == "dve" for x in js)
        jobs = self.jobs(i, last)
        at = [x[:2] for x in jobs].index(key)
        assert jobs[at][2] == "dve"
        here = count(jobs[: at + 1])
        return here if i is None else i * count(self.loop) + (count(self.pro) + here)

    def freed_ahead(self, i):
        count = lambda js: sum(x[2] == "dve" for x in js)
        return i * count(self.loop) + count(self.pro)

    def freed_by_act(self, i):
        count = lambda js: sum(x[2] == "act" for x in js)
        return i * count(self.loop) + count(self.pro)

    def before(self, i, last, key):
        jobs = self.jobs(i, last)
        at = [x[:2] for x in jobs].index(key) - 2
        count = lambda js, who: sum(x[2] == who for x in js)
        if i is None:
            if at < 0:
                return None
            who = jobs[at][2]
            return who, count(jobs[: at + 1], who)
        if at >= 0:
            who = jobs[at][2]
            return who, i * count(self.loop, who) + (count(self.pro, who) + count(jobs[: at + 1], who))
        who = self.loop[at][2]
        return who, i * count(self.loop, who) + (count(self.pro, who) - count(self.loop[len(self.loop) + at + 1:], who))


class Steps:

    def __init__(self, eng, sem, base, i, per):
        self.eng, self.sem, self.n, self.i, self.per = eng, sem, base, i, per

    def value(self):
        return self.n if self.i is None else self.i * self.per + self.n

    def inc(self, ins):
        self.n += 1
        ins.then_inc(self.sem, 1)

    def wait(self):
        self.eng.wait_ge(self.sem, self.value())


def cross_attention(nc, x, xT, ctx, ctxT, mask0, mask1, mask0T, mask1T,
                    Wq0T, bq, Wk0T, bk, Wv0T, bv, Wo0T, bo, ln_g, ln_b,
                    Wq1T, Wo1T, gamma, beta, ident, headmask, halves, quarters, out):
    banks = Banks()
    stack = ExitStack()
    with stack:
        def sb(name, shape, dt=F32):
            return stack.enter_context(nc.sbuf_tensor(name, shape, dt))

        def psum(name, shape, dt=F32):
            return stack.enter_context(nc.psum_tensor(name, shape, dt))

        def sem(name):
            return stack.enter_context(nc.semaphore(name))

        vals = sb("vals", [P, 2 * J * VB + 1, 32])
        ONES = 2 * J * VB
        e_flat = vals[:, 0:J * VB, :].rearrange("p n c -> p (n c)")
        e_raw = e_flat[:, 0:KT * T].rearrange("p (k t) -> p k t", k=KT)
        a_flat = vals[:, J * VB:2 * J * VB, :].rearrange("p n c -> p (n c)")
        xt_hi = sb("xt_hi", [P, KT, T], F32R)
        xt_lo = sb("xt_lo", [P, KT, T], F32R)
        key_hi = sb("key_hi", [P, 2, T], F32R)
        key_lo = sb("key_lo", [P, 2, T], F32R)
        wk_hi = sb("wk_hi", [P, KT, H], F32R)
        wk_lo = sb("wk_lo", [P, KT, H], F32R)
        wv_hi = sb("wv_hi", [P, KT, H], F32R)
        wv_lo = sb("wv_lo", [P, KT, H], F32R)
        wq1 = sb("wq1", [P, KT, H])
        wo = sb("wo", [P, KT, H])
        raw = sb("raw", [P, T])
        q_hi = sb("q_hi", [P, KT, S], F32R)
        q_lo = sb("q_lo", [P, KT, S])
        blk_hi = sb("blk_hi", [P, 2, HU, S], F32R)
        blk_lo = sb("blk_lo", [P, 2, HU, S], F32R)
        shift = sb("shift", [PW, 2, W], F32R)
        chunk_max = sb("chunk_max", [PW, 2, PAIRS, NC])
        minus_max = sb("minus_max", [PW, 2, PAIRS])
        bias_row = sb("bias_row", [PW, T], BF16)
        bias_col = sb("bias_col", [TP, 2, B, J])
        bias_now = sb("bias_now", [TP, 2, J])
        probs = sb("probs", [P, RING * W])
        norm = probs[0:S, 0:H]
        resid = sb("resid", [S, H])
        g_row = sb("g_row", [S, H])
        b_row = sb("b_row", [S, H])
        bo_row = sb("bo_row", [S, H])
        sums = sb("sums", [P, W])
        numer = sb("numer", [P, PW])
        recip = sb("recip", [P, PW])
        half0 = numer[:, 0:S]
        attn = sb("attn", [P, KT, S])
        zT = sums[:, 0:KT * S].rearrange("p (k s) -> p k s", k=KT)
        cols = sb("cols", [P, 5, KT])
        bq_raw = sb("bq_raw", [P, KT])
        stats = sb("stats", [S, 6])
        mv = sb("mv", [S, 2, 2])
        rstd = sb("rstd", [S, 2, 1])
        vpe = sb("vpe", [S, 2, 1])
        minus_half = sb("minus_half", [S, 1])
        ident_sb = sb("ident_sb", [PW, PW])
        ones_r = sb("ones_r", [PW, TP], F32R)
        quarter = sb("quarter", [P, CG])
        hmask = sb("hmask", [P, HU])
        hsel = sb("hsel", [P, 2])

        sc_ps = [psum(f"sc_ps{n}", [P, 512]) for n in range(2)]
        max_ps = [psum(f"max_ps{n}", [P, 512]) for n in range(2)]
        pv_ps = psum("pv_ps", [P, 512])
        sum_ps = psum("sum_ps", [P, 512])
        job_ps = [psum(f"job_ps{n}", [P, 512]) for n in range(2)]

        q0_dram = nc.dram_tensor("queries0", [P, KT, B * S], F32, kind="Internal").ap()
        bias_dram = nc.dram_tensor("bias_rows", [2, B * J, TP], BF16, kind="Internal").ap()

        s_consts = sem("s_consts")
        s_weights = sem("s_weights")
        s_xT = sem("s_xT")
        s_wo = sem("s_wo")
        s_first = sem("s_first")
        s_raw = sem("s_raw")
        s_ctx = sem("s_ctx")
        s_x = sem("s_x")
        s_maskin = sem("s_maskin")
        s_biasout = sem("s_biasout")
        s_bias = sem("s_bias")
        s_out = sem("s_out")
        s_fill = sem("s_fill")
        s_w_hi = sem("s_w_hi")
        s_w_lo = sem("s_w_lo")
        s_bq = sem("s_bq")
        s_mask = sem("s_mask")
        s_job = sem("s_job")
        s_free_act = sem("s_free_act")
        s_free_dve = sem("s_free_dve")
        s_key_hi = sem("s_key_hi")
        s_split_hi = sem("s_split_hi")
        s_split_lo = sem("s_split_lo")
        s_q0out = sem("s_q0out")
        s_q0in = sem("s_q0in")
        s_q = sem("s_q")
        s_blk = sem("s_blk")
        s_max = sem("s_max")
        s_red = sem("s_red")
        s_rowmax = sem("s_rowmax")
        s_shift = sem("s_shift")
        s_score = sem("s_score")
        s_exp = sem("s_exp")
        s_pv = sem("s_pv")
        s_sums = sem("s_sums")
        s_attn = sem("s_attn")
        s_dve = sem("s_dve")
        s_bnow = sem("s_bnow")
        s_passed = sem("s_passed")
        s_resid = sem("s_resid")
        s_var = sem("s_var")
        s_rstd = sem("s_rstd")
        s_norm = sem("s_norm")
        s_zT = sem("s_zT")

        N_SC = U * J
        N_UNIT = PAIRS * NC
        N_RED = U * N_UNIT
        L_RED = UL * N_UNIT
        DVE_STEPS = U * 2 + 7
        CONSTS = 13 * 16

        q0_all = a_flat[:, 0:KT * B * S].rearrange("p (k n) -> p k n", k=KT)
        xT_sb = wo[:, :, :].rearrange("p k n -> p (k n)")[:, 0:KT * B * S].rearrange("p (k n) -> p k n", k=KT)
        m0 = B * J
        mask_cols = [probs[0:TP, 0:m0].bitcast(I32), probs[0:TP, 240:240 + m0 // 4].bitcast(U8)]
        mask_rows = [probs[0:m0, 100:100 + TP].bitcast(I32), probs[0:m0, 280:280 + 32].bitcast(U8)[:, 0:TP]]
        bias_bf = probs[0:m0, 600:600 + TP].bitcast(BF16).rearrange("p (l t) -> p l t", l=2)
        L0_KEYS = UL * NC

        block = stack.enter_context(nc.Block())


        LOADS = 2 * PARTS
        SPLITS = LOADS * PARTS

        def part_of(n, step):
            t = slice(step * PT, (step + 1) * PT)
            if n < PARTS:
                return raw[:, t], key_hi[:, n % 2, t], key_lo[:, n % 2, t]
            return raw[:, t], xt_hi[:, n - PARTS, t], xt_lo[:, n - PARTS, t]

        def place_free(eng, i, last, n):
            if n < 2:
                eng.wait_ge(s_score, i * N_SC + (n + 3) * J)
            elif n < PARTS:
                eng.wait_ge(s_job, banks.done(i, last, ("V", JV * (n - 1) - 1)))
            else:
                eng.wait_ge(s_score, i * N_SC + (UL + 1 + n - PARTS) * J)

        def par(u):
            return u % 2

        @block.sync
        def _(sp):
            for src, dst in ((mask0, mask_cols[0]), (mask1, mask_cols[1]), (mask0T, mask_rows[0]), (mask1T, mask_rows[1])):
                sp.dma_start(dst, src).then_inc(s_maskin, 16)
            for dst, src in ((a_flat[:, 0:2048], Wk0T), (a_flat[:, 2048:4096], Wv0T), (a_flat[:, 4096:6144], Wq0T)):
                sp.dma_start(dst.rearrange("p (k n) -> p k n", k=KT), src.rearrange("(k p) n -> p k n", p=P)).then_inc(s_weights, 16)
            sp.dma_start(xT_sb, xT.rearrange("(k p) n -> p k n", p=P)).then_inc(s_xT, 16)
            sp.dma_start(e_raw, ctxT[0].rearrange("(k p) t -> p k t", p=P)).then_inc(s_first, 16)
            smalls = ((bq_raw[:, :], bq), (cols[:, 1, :], bk), (cols[:, 2, :], bv), (cols[:, 3, :], gamma),
                      (cols[:, 4, :], beta), (ident_sb[:, :], ident),
                      (hmask[:, :], headmask), (hsel[:, :], halves), (quarter[:, :], quarters))
            for dst, src in smalls:
                sp.dma_start(dst, src).then_inc(s_consts, 16)
            for dst, src in ((g_row, ln_g), (b_row, ln_b), (bo_row, bo)):
                sp.dma_start(dst[:, :], src.partition_broadcast(S)).then_inc(s_consts, 16)
            sp.dma_start(wq1[:, :, :], Wq1T.rearrange("(k p) n -> p k n", p=P)).then_inc(s_consts, 16)
            sp.wait_ge(s_mask, 4)
            for layer in range(2):
                sp.dma_start(bias_dram[layer], bias_bf[:, layer, :]).then_inc(s_biasout, 16)
            sp.wait_ge(s_biasout, 32)
            sp.dma_start(bias_row[:, :], bias_dram[0, 0:J, :].rearrange("j p -> (j p)").partition_broadcast(PW)).then_inc(s_bias, 16)
            sp.wait_ge(s_job, banks.done(None, False, ("Q", KT - 1)))
            sp.dma_start(wo[:, :, :], Wo0T.rearrange("(k p) n -> p k n", p=P)).then_inc(s_wo, 16)
            sp.dma_start(resid[:, :], x[0]).then_inc(s_x, 16)
            sp.wait_ge(s_free_act, KT)
            sp.dma_start(q0_dram, q0_all).then_inc(s_q0out, 16)
            sp.wait_ge(s_q0out, 16)
            sp.dma_start(q_lo[:, :, :], q0_dram[:, :, 0:S]).then_inc(s_q0in, 16)
            sp.wait_ge(s_w_lo, 2)
            sp.dma_start(a_flat[0:TP, :], ctx[0].rearrange("(p j) d -> p (j d)", j=J)).then_inc(s_ctx, 16)

            def load_part(i, n):
                sp.wait_ge(s_split_lo, i * SPLITS + (n + PARTS) * PARTS)
                if n < PARTS:
                    src = ctxT[i + 1, :, n * PT:(n + 1) * PT].rearrange("(k p) t -> p k t", p=P)
                    sp.dma_start(raw[:, :].rearrange("p (k t) -> p k t", k=KT), src).then_inc(s_raw, 16)
                else:
                    ct = n - PARTS
                    sp.dma_start(raw[:, :], ctxT[i + 1, ct * P:(ct + 1) * P, :]).then_inc(s_raw, 16)

            def batch(i, last):
                if not last:
                    load_part(i, 0)
                sp.wait_ge(s_red, i * N_RED + L_RED)
                sp.dma_start(bias_row[:, :], bias_dram[1, bass.ts(i, J), :].rearrange("j p -> (j p)").partition_broadcast(PW)).then_inc(s_bias, 16)
                if not last:
                    load_part(i, 1)
                    load_part(i, 2)
                sp.wait_ge(s_job, banks.done(i, last, ("out", 0)))
                sp.dma_start(wo[:, :, :], Wo1T.rearrange("(k p) n -> p k n", p=P)).then_inc(s_wo, 16)
                if not last:
                    load_part(i, 3)
                    load_part(i, 4)
                    load_part(i, 5)
                    load_part(i, 6)
                    sp.wait_ge(s_red, i * N_RED + N_RED)
                    sp.dma_start(bias_row[:, :], bias_dram[0, bass.ts(i + 1, J), :].rearrange("j p -> (j p)").partition_broadcast(PW)).then_inc(s_bias, 16)
                    sp.wait_ge(s_blk, (i * U + U) * 2)
                    sp.dma_start(q_lo[:, :, :], q0_dram[:, :, bass.ts(i + 1, S)]).then_inc(s_q0in, 16)
                    load_part(i, 7)
                    sp.wait_ge(s_pv, (i + 1) * N_SC)
                    sp.dma_start(a_flat[0:TP, :], ctx[i + 1].rearrange("(p j) d -> p (j d)", j=J)).then_inc(s_ctx, 16)
                sp.wait_ge(s_free_dve, banks.freed(i, last, ("out", 1)))
                sp.dma_start(out[i], resid[:, :]).then_inc(s_out, 16)
                if not last:
                    sp.dma_start(wo[:, :, :], Wo0T.rearrange("(k p) n -> p k n", p=P)).then_inc(s_wo, 16)
                    sp.wait_ge(s_out, i * 16 + 16)
                    sp.dma_start(resid[:, :], x[i + 1]).then_inc(s_x, 16)

            with sp.Fori(0, B - 1) as i:
                batch(i, False)
            batch(B - 1, True)
            sp.wait_ge(s_out, B * 16)

        @block.tensor
        def _(pe):
            def take_bank(i, last, key):
                if (need := banks.before(i, last, key)) is not None:
                    pe.wait_ge(s_free_act if need[0] == "act" else s_free_dve, need[1])
                return job_ps[banks.slot(i, last, key)]

            def split_product(dst, terms, more=False):
                for n, (a, b) in enumerate(terms):
                    mm = pe.matmul(dst, a, b, start=n == 0, stop=n == len(terms) - 1 and not more)
                return mm

            def project_key(i, last, n):
                ct, c = divmod(n, NC)
                bank = take_bank(i, last, ("K", n))
                w = slice(ct * P, (ct + 1) * P)
                t = slice(c * CW, (c + 1) * CW)
                for k in range(KT):
                    if i is not None and ct == 0 and c == 0:
                        pe.wait_ge(s_split_lo, i * SPLITS + (PARTS + PARTS + k + 1) * PARTS)
                    for m, (a, b) in enumerate(((wk_hi[:, k, w], xt_hi[:, k, t]), (wk_hi[:, k, w], xt_lo[:, k, t]),
                                                (wk_lo[:, k, w], xt_hi[:, k, t]))):
                        mm = pe.matmul(bank[:, 0:CW], a, b, start=k == 0 and m == 0, stop=k == KT - 1 and m == 2)
                mm.then_inc(s_job, 1)

            def project_value(i, last, j):
                bank = take_bank(i, last, ("V", j))
                if i is None:
                    hi, lo, t = xt_hi, xt_lo, slice(j * TP, (j + 1) * TP)
                else:
                    n = j // JV
                    pe.wait_ge(s_split_lo, i * SPLITS + (n + 1 + PARTS) * PARTS)
                    hi, lo = (x[:, n % 2, :].rearrange("p (k t) -> p k t", k=KT) for x in (key_hi, key_lo))
                    t = slice((j % JV) * TP, (j % JV + 1) * TP)
                terms = []
                for k in range(KT):
                    terms += [(hi[:, k, t], wv_hi[:, k, :]), (hi[:, k, t], wv_lo[:, k, :]), (lo[:, k, t], wv_hi[:, k, :])]
                split_product(bank[0:TP, :], terms).then_inc(s_job, 1)

            def max_rows(i, u, first, count):
                for n in range(first, first + count):
                    c, p = divmod(n, PAIRS)
                    if n == 0:
                        pe.wait_ge(s_blk, (i * U + (u + 1)) * 2)
                    if p == 0 and u % U < UL:
                        pe.wait_ge(s_key_hi, i * L0_KEYS + ((u // U) * L0_KEYS + (u % U * NC + c + 1)))
                    keys = key_hi[:, par(u), :] if u % U < UL else xt_hi[:, u % U - UL, :]
                    q = blk_hi[:, par(u), 2 * p:2 * p + 2, :].rearrange("p h s -> p (h s)")
                    m = u * N_UNIT + n
                    if not (isinstance(i, int) and i == 0 and m < 2):
                        pe.wait_ge(s_red, i * N_RED + (m - 1))
                    pe.matmul(max_ps[m % 2][0:PW, 0:CW], q, keys[:, c * CW:(c + 1) * CW], start=True, stop=True).then_inc(s_max, 1)

            def score(i, last, u, j):
                n = u * J + j
                if n >= 2:
                    pe.wait_ge(s_exp, i * N_SC + (n - 1))
                if j == 0:
                    pe.wait_ge(s_shift, i * U + (u + 1))
                    if u < UL:
                        pe.wait_ge(s_free_dve, banks.freed(i, last, ("K", u * NC + NC - 1)) if u else banks.freed_ahead(i))
                t = slice(j * TP, (j + 1) * TP)
                if u < UL:
                    hi, lo = key_hi[:, par(u), t], key_lo[:, par(u), t]
                else:
                    hi, lo = xt_hi[:, u - UL, t], xt_lo[:, u - UL, t]
                qh = blk_hi[:, par(u), :, :].rearrange("p h s -> p (h s)")
                ql = blk_lo[:, par(u), :, :].rearrange("p h s -> p (h s)")
                terms = [(hi, qh), (hi, ql), (lo, qh), (ones_r[:, :], shift[:, par(u), :])]
                split_product(sc_ps[n % 2][0:TP, 0:W], terms).then_inc(s_score, 1)

            def weigh(i, u, j):
                n = u * J + j
                pe.wait_ge(s_exp, i * N_SC + (n + 1))
                if j == 0:
                    if u:
                        pe.wait_ge(s_sums, (i * U + u) * 2)
                    if u == 0:
                        pe.wait_ge(s_free_act, banks.freed_by_act(i))
                    if u == UL:
                        pe.wait_ge(s_ctx, i * 16 + 16)
                ring = (n % RING) * W
                for p in range(PAIRS):
                    v0 = (u % UL) * PAIRS + p + (0 if u < UL else J * VB) + j * VB
                    pe.matmul(pv_ps[CG * p:CG * p + CG, 0:PW], vals[0:TP, v0, :], probs[0:TP, ring + p * PW:ring + (p + 1) * PW],
                              start=j == 0, stop=j == J - 1, skip_group_check=True, tile_position=(0, CG * p))
                q0 = CG * (j % 4)
                pe.matmul(sum_ps[q0:q0 + CG, 0:W], vals[0:TP, ONES, :], probs[0:TP, ring:ring + W],
                          start=j < 4, stop=j >= J - 4, skip_group_check=True, tile_position=(0, q0)).then_inc(s_pv, 1)

            def total(i, last, u):
                bank = take_bank(i, last, ("sum", u))
                pe.wait_ge(s_sums, (i * U + (u + 1)) * 2)
                for p in range(PAIRS):
                    mm = pe.matmul(bank[CG * p:CG * p + CG, 0:PW], quarter[:, :], sums[:, p * PW:(p + 1) * PW],
                                   start=True, stop=True, tile_position=(0, CG * p))
                mm.then_inc(s_job, 1)

            def output(i, last, layer):
                bank = take_bank(i, last, ("out", layer))
                pe.wait_ge(s_attn, i * U + (layer + 1) * UL)
                pe.wait_ge(s_wo, i * 32 + 16 * (layer + 1))
                for k in range(KT):
                    mm = pe.matmul(bank[0:S, :], attn[:, k, :], wo[:, k, :], start=k == 0, stop=k == KT - 1)
                mm.then_inc(s_job, 1)

            def main_pass(i, last, u):
                for j in range(J):
                    score(i, last, u, j)
                    if (u % UL, j) != (0, 0):
                        weigh(i, u - (j == 0), (j - 1) % J)
                    if u % UL != UL - 1:
                        if j in K_AT and u < UL:
                            project_key(i, last, (u + 1) * NC + K_AT[j])
                        if j in MAX_AT[u // UL]:
                            at = MAX_AT[u // UL]
                            max_rows(i, u + 1, sum(at[x] for x in at if x < j), at[j])
                    if j == SUM_AT and u % UL:
                        total(i, last, u - 1)
                if u % UL == UL - 1:
                    weigh(i, u, J - 1)

            def to_layer1(i, last):
                pe.wait_ge(s_consts, CONSTS)
                bank = take_bank(i, last, ("z", 0))
                pe.wait_ge(s_norm, i + 1)
                pe.sem_inc(s_passed, 1)
                for k in range(KT):
                    mm = pe.transpose(bank[:, k * S:(k + 1) * S], norm[:, k * P:(k + 1) * P], ident_sb[0:S, 0:S])
                mm.then_inc(s_job, 1)

            def queries1(i, last):
                bank = take_bank(i, last, ("Q1", 0))
                pe.wait_ge(s_zT, i + 1)
                for ct in range(KT):
                    for k in range(KT):
                        mm = pe.matmul(bank[:, ct * S:(ct + 1) * S], wq1[:, k, ct * P:(ct + 1) * P], zT[:, k, :],
                                       start=k == 0, stop=k == KT - 1)
                mm.then_inc(s_job, 1)

            def between(i, last, plan, u):
                first = 0
                for x in plan:
                    if isinstance(x, int):
                        max_rows(i, u, first, x)
                        first += x
                    elif x[0] == "V":
                        if not last:
                            project_value(i, last, x[1])
                    elif x[0] == "K":
                        project_key(i, last, x[1])
                    elif x[0] == "sum":
                        total(i, last, x[1])
                    elif x[0] == "out":
                        output(i, last, x[1])
                    elif x[0] == "z":
                        to_layer1(i, last)
                    else:
                        queries1(i, last)

            pe.wait_ge(s_weights, 48)
            pe.wait_ge(s_xT, 16)
            wq0 = a_flat[:, 4096:6144].rearrange("p (k n) -> p k n", k=KT)
            for ct in range(KT):
                bank = take_bank(None, False, ("Q", ct))
                for k in range(KT):
                    mm = pe.matmul(bank[:, 0:B * S], wq0[:, k, ct * P:(ct + 1) * P], xT_sb[:, k, :], start=k == 0, stop=k == KT - 1)
                mm.then_inc(s_job, 1)
            pe.wait_ge(s_w_hi, 2)
            pe.wait_ge(s_w_lo, 2)
            pe.wait_ge(s_split_lo, KT * PARTS)
            pe.wait_ge(s_q0out, 16)
            for j in range(J - 1):
                project_value(None, False, j)
            for c in range(NC):
                project_key(None, False, c)
            project_value(None, False, J - 1)
            pe.wait_ge(s_fill, 3)
            max_rows(0, 0, 0, N_UNIT)

            def batch(i, last):
                for u in range(UL):
                    main_pass(i, last, u)
                between(i, last, BETWEEN_LAYERS, UL)
                for u in range(UL, U):
                    main_pass(i, last, u)
                if last:
                    total(i, last, U - 1)
                    output(i, last, 1)
                else:
                    between(i, last, BETWEEN_BATCHES, U)

            with pe.Fori(0, B - 1) as i:
                batch(i, False)
            batch(B - 1, True)

        @block.scalar
        def _(act):
            def key_hi_part(i, last, n):
                ct, c = divmod(n, NC)
                act.wait_ge(s_job, banks.done(i, last, ("K", n)))
                nc.scalar.activation(key_hi[:, par(ct), c * CW:(c + 1) * CW], job_ps[banks.slot(i, last, ("K", n))][:, 0:CW],
                                     ACT.Identity, bias=cols[:, 1, ct:ct + 1]).then_inc(s_key_hi, 1)

            def split_hi(i, last, n, step):
                if step == 0:
                    act.wait_ge(s_raw, i * (16 * LOADS) + 16 * (n + 1))
                    place_free(act, i, last, n)
                src, hi, _ = part_of(n, step)
                nc.scalar.activation(hi, src, ACT.Copy).then_inc(s_split_hi, 1)

            def value_tile(i, last, j):
                act.wait_ge(s_job, banks.done(i, last, ("V", j)))
                nc.scalar.activation(e_flat[0:TP, j * H:(j + 1) * H], job_ps[banks.slot(i, last, ("V", j))][0:TP, :],
                                     ACT.Copy).then_inc(s_free_act, 1)

            def copy_sums(i, last, u):
                act.wait_ge(s_pv, i * N_SC + (u + 1) * J)
                act.wait_ge(s_job, banks.done(i, last, ("sum", u - 1)) if u else i * len(banks.loop) + len(banks.pro))
                if u:
                    act.wait_ge(s_attn, i * U + u)
                else:
                    act.wait_ge(s_free_dve, banks.freed_ahead(i))
                nc.scalar.activation(numer[:, :], pv_ps[:, 0:PW], ACT.Copy).then_inc(s_sums, 1)
                nc.scalar.activation(sums[:, :], sum_ps[:, 0:W], ACT.Copy).then_inc(s_sums, 1)

            act.wait_ge(s_bq, 1)
            act.wait_ge(s_consts, CONSTS)
            act.wait_ge(s_w_lo, 1)
            for ct in range(KT):
                act.wait_ge(s_job, banks.done(None, False, ("Q", ct)))
                nc.scalar.activation(q0_all[:, ct, :], job_ps[banks.slot(None, False, ("Q", ct))][:, 0:B * S], ACT.Identity,
                                     bias=cols[:, 0, ct:ct + 1], scale=SCALE).then_inc(s_free_act, 1)
            act.wait_ge(s_first, 16)
            for k in range(KT):
                for n in range(PARTS):
                    t = slice(n * PT, (n + 1) * PT)
                    nc.scalar.activation(xt_hi[:, k, t], e_raw[:, k, t], ACT.Copy).then_inc(s_split_hi, 1)
            for j in range(J - 1):
                value_tile(None, False, j)
            for n in range(NC):
                key_hi_part(None, False, n)
            value_tile(None, False, J - 1)

            def batch(i, last):
                for u in range(U):
                    layer = u // UL
                    if u % UL == 0:
                        act.wait_ge(s_bnow, i * 2 + (layer + 1))
                    for j in range(J):
                        if j == 1 and u % UL:
                            copy_sums(i, last, u - 1)
                        n = u * J + j
                        act.wait_ge(s_score, i * N_SC + (n + 1))
                        if n >= RING:
                            act.wait_ge(s_pv, i * N_SC + (n + 1 - RING))
                        if u == UL and j == 0:
                            act.wait_ge(s_job, banks.done(i, last, ("z", 0)))
                        nc.scalar.activation(probs[0:TP, (n % RING) * W:(n % RING + 1) * W], sc_ps[n % 2][0:TP, 0:W],
                                             ACT.Exp, bias=bias_now[:, layer, j:j + 1]).then_inc(s_exp, 1)
                        if j in K_AT and u < UL - 1:
                            key_hi_part(i, last, (u + 1) * NC + K_AT[j])
                        if j in SPLIT_AT and u in SPLIT_OF and not last:
                            split_hi(i, last, SPLIT_OF[u], SPLIT_AT[j])
                    if u == UL - 1:
                        copy_sums(i, last, u)
                        if not last:
                            value_tile(i, last, 0)
                            for step in range(PARTS):
                                split_hi(i, last, 1, step)
                            for j in range(1, JV + 1):
                                value_tile(i, last, j)
                            for step in range(PARTS):
                                split_hi(i, last, 2, step)
                            for j in range(JV + 1, 3 * JV):
                                value_tile(i, last, j)
                if last:
                    copy_sums(i, last, U - 1)
                    return
                for step in range(PARTS):
                    split_hi(i, last, LOADS - 1, step)
                copy_sums(i, last, U - 1)
                for j in range(3 * JV, J - 1):
                    value_tile(i, last, j)
                for n in range(NC):
                    key_hi_part(i, last, n)
                value_tile(i, last, J - 1)

            with act.Fori(0, B - 1) as i:
                batch(i, False)
            batch(B - 1, True)

        @block.vector
        def _(dve):
            def key_lo_part(i, last, n):
                ct, c = divmod(n, NC)
                t = slice(c * CW, (c + 1) * CW)
                dve.wait_ge(s_key_hi, n + 1 if i is None else i * L0_KEYS + ((ct == 0) * L0_KEYS + n + 1))
                nc.vector.scalar_tensor_tensor(out=key_lo[:, par(ct), t], in0=job_ps[banks.slot(i, last, ("K", n))][:, 0:CW],
                                               scalar=cols[:, 1, ct:ct + 1], in1=key_hi[:, par(ct), t].bitcast(F32),
                                               op0=ALU.add, op1=ALU.subtract).then_inc(s_free_dve, 1)

            def split_lo(i, last, n, step):
                src, hi, lo = part_of(n, step)
                dve.wait_ge(s_split_hi, i * SPLITS + ((n + PARTS) * PARTS + step + 1))
                nc.vector.tensor_tensor(lo, src, hi.bitcast(F32), ALU.subtract).then_inc(s_split_lo, 1)

            def take_max(i, u, first, count):
                for n in range(first, first + count):
                    c, p = divmod(n, PAIRS)
                    m = u * N_UNIT + n
                    if n == 0:
                        if not (isinstance(i, int) and i == 0 and u == 0):
                            dve.wait_ge(s_shift, i * U + u)
                        dve.wait_ge(s_bias, i * 32 + 16 * (1 + u // UL))
                    dve.wait_ge(s_max, i * N_RED + (m + 1))
                    dve.sem_inc(s_passed, 1)
                    at = max_ps[m % 2][0:PW, 0:CW]
                    nc.vector.tensor_tensor_reduce(out=at, in0=at, in1=bias_row[:, c * CW:(c + 1) * CW], scale=1.0, scalar=FLOOR,
                                                   op0=ALU.add, op1=ALU.max, accum_out=chunk_max[:, par(u), p, c:c + 1]).then_inc(s_red, 1)
                    if n == N_UNIT - 1:
                        dve.wait_ge(s_red, i * N_RED + (m + 1))
                        nc.vector.tensor_reduce(minus_max[:, par(u), :], chunk_max[:, par(u), :, :], mybir.AxisListType.X, ALU.max, negate=True).then_inc(s_rowmax, 1)

            def divide(i, last, u, step):
                dve.wait_ge(s_job, banks.done(i, last, ("sum", u)))
                nc.vector.reciprocal(recip[:, :], job_ps[banks.slot(i, last, ("sum", u))][:, 0:PW]).then_inc(s_free_dve, 1)
                dve.wait_ge(s_free_dve, banks.freed(i, last, ("sum", u)))
                step.inc(nc.vector.tensor_tensor(recip[:, :], numer[:, :], recip[:, :], ALU.mult))
                step.wait()
                ct = u % UL
                step.inc(nc.vector.tensor_scalar(half0[:, :], recip[:, 0:S], hsel[:, 0:1], cols[:, 2, ct:ct + 1] if u < UL else 0.0,
                                                 ALU.mult, ALU.add))
                step.wait()
                nc.vector.scalar_tensor_tensor(out=attn[:, ct, :], in0=recip[:, S:2 * S], scalar=hsel[:, 1:2], in1=half0[:, :],
                                               op0=ALU.mult, op1=ALU.add).then_inc(s_attn, 1)

            def layer_norm(i, n, src, dst, step):
                step.inc(nc.vector.bn_stats(stats[:, :], src))
                step.wait()
                dve.sem_inc(s_passed, 1)
                step.inc(nc.vector.bn_aggr(mv[:, n, :], stats[:, :]))
                step.wait()
                nc.vector.tensor_scalar(vpe[:, n, :], mv[:, n, 1:2], EPS, None, ALU.add).then_inc(s_var, 1)
                dve.wait_ge(s_rstd, i * 2 + (n + 1))
                return nc.vector.tensor_scalar(dst, src, mv[:, n, 0:1], rstd[:, n, :], ALU.subtract, ALU.mult)

            nc.vector.memset(vals[:, ONES, :], 1.0).then_inc(s_fill, 1)
            nc.vector.memset(ones_r[:, :].bitcast(F32), 1.0).then_inc(s_fill, 1)
            nc.vector.memset(minus_half[:, :], -0.5).then_inc(s_fill, 1)
            dve.wait_ge(s_maskin, 64)
            for layer in range(2):
                nc.vector.tensor_scalar(bias_col[:, layer, :, :].rearrange("p b j -> p (b j)"), mask_cols[layer], 0.0, MASKED, ALU.is_equal, ALU.mult).then_inc(s_mask, 1)
                nc.vector.tensor_scalar(bias_bf[:, layer, :], mask_rows[layer], 0.0, MASKED, ALU.is_equal, ALU.mult).then_inc(s_mask, 1)
            dve.wait_ge(s_mask, 4)
            nc.vector.tensor_copy(bias_now[:, 0, :], bias_col[:, 0, 0, :]).then_inc(s_bnow, 1)
            dve.wait_ge(s_consts, CONSTS)
            nc.vector.tensor_scalar(cols[:, 0, :], bq_raw[:, :], SCALE, None, ALU.mult).then_inc(s_bq, 1)
            dve.wait_ge(s_weights, 48)
            for n, (hi, lo) in enumerate(((wk_hi, wk_lo), (wv_hi, wv_lo))):
                raw = a_flat[:, n * 2048:(n + 1) * 2048].rearrange("p (k n) -> p k n", k=KT)
                nc.vector.tensor_copy(hi[:, :, :], raw).then_inc(s_w_hi, 1)
                dve.wait_ge(s_w_hi, n + 1)
                nc.vector.tensor_tensor(lo[:, :, :], raw, hi[:, :, :].bitcast(F32), ALU.subtract).then_inc(s_w_lo, 1)
            dve.wait_ge(s_first, 16)
            for k in range(KT):
                for n in range(PARTS):
                    t = slice(n * PT, (n + 1) * PT)
                    dve.wait_ge(s_split_hi, k * PARTS + n + 1)
                    nc.vector.tensor_tensor(xt_lo[:, k, t], e_raw[:, k, t], xt_hi[:, k, t].bitcast(F32), ALU.subtract).then_inc(s_split_lo, 1)

            def queries0(i, count):
                dve.wait_ge(s_q0in, i * 16 + 16)
                nc.vector.tensor_copy(q_hi[:, :, :], q_lo[:, :, :]).then_inc(s_q, 1)
                dve.wait_ge(s_q, count + 1)
                nc.vector.tensor_tensor(q_lo[:, :, :], q_lo[:, :, :], q_hi[:, :, :].bitcast(F32), ALU.subtract).then_inc(s_q, 1)

            queries0(0, 0)
            for n in range(NC):
                key_lo_part(None, False, n)
            take_max(0, 0, 0, N_UNIT)

            def batch(i, last):
                step = Steps(dve, s_dve, 0, i, DVE_STEPS)
                for u in range(U):
                    if u == U - 1 and not last:
                        queries0(i + 1, i * 3 + 3)
                    for j in range(J):
                        if u % UL != UL - 1 and j in K_AT and u < UL:
                            key_lo_part(i, last, (u + 1) * NC + K_AT[j])
                        if j in SPLIT_AT and u in SPLIT_OF and not last:
                            split_lo(i, last, SPLIT_OF[u], SPLIT_AT[j])
                        if u % UL != UL - 1 and j in MAX_AT[u // UL]:
                            at = MAX_AT[u // UL]
                            take_max(i, u + 1, sum(at[x] for x in at if x < j), at[j])
                        if j == SUM_AT and u % UL:
                            divide(i, last, u - 1, step)
                    if u == 1:
                        nc.vector.tensor_copy(bias_now[:, 1, :], bias_col[:, 1, bass.ds(i, 1), :].rearrange("p b j -> p (b j)")).then_inc(s_bnow, 1)
                    if u == UL + 1 and not last:
                        dve.wait_ge(s_exp, i * N_SC + UL * J)
                        nc.vector.tensor_copy(bias_now[:, 0, :], bias_col[:, 0, bass.ds(i + 1, 1), :].rearrange("p b j -> p (b j)")).then_inc(s_bnow, 1)
                    if u == UL - 1:
                        between_layers(i, last, step)
                if last:
                    divide(i, last, U - 1, step)
                    finish(i, last)
                else:
                    for n in range(PARTS):
                        split_lo(i, last, LOADS - 1, n)
                    divide(i, last, U - 1, step)
                    finish(i, last)
                    key_lo_part(i, last, 0)
                    key_lo_part(i, last, 1)
                    take_max(i, U, 0, 2)
                    key_lo_part(i, last, 2)
                    take_max(i, U, 2, N_UNIT - 2)
                assert step.n == DVE_STEPS, step.n

            def between_layers(i, last, step):
                divide(i, last, UL - 1, step)
                if not last:
                    for n in range(PARTS):
                        split_lo(i, last, 1, n)
                dve.wait_ge(s_resid, i + 1)
                dve.wait_ge(s_job, banks.done(i, last, ("out", 0)))
                nc.vector.tensor_tensor(resid[:, :], job_ps[banks.slot(i, last, ("out", 0))][0:S, :], resid[:, :], ALU.add).then_inc(s_free_dve, 1)
                dve.wait_ge(s_free_dve, banks.freed(i, last, ("out", 0)))
                step.inc(layer_norm(i, 0, resid[:, :], resid[:, :], step))
                step.wait()
                step.inc(nc.vector.tensor_tensor(resid[:, :], resid[:, :], g_row[:, :], ALU.mult))
                step.wait()
                step.inc(nc.vector.tensor_tensor(resid[:, :], resid[:, :], b_row[:, :], ALU.add))
                step.wait()
                layer_norm(i, 1, resid[:, :], norm, step).then_inc(s_norm, 1)
                dve.wait_ge(s_job, banks.done(i, last, ("z", 0)))
                bank = job_ps[banks.slot(i, last, ("z", 0))][:, 0:KT * S].rearrange("p (k s) -> p k s", k=KT)
                nc.vector.tensor_tensor(zT[:, :, :], bank, cols[:, 3, :].unsqueeze(2).to_broadcast([P, KT, S]), ALU.mult).then_inc(s_free_dve, 1)
                dve.wait_ge(s_free_dve, banks.freed(i, last, ("z", 0)))
                nc.vector.tensor_tensor(zT[:, :, :], zT[:, :, :], cols[:, 4, :].unsqueeze(2).to_broadcast([P, KT, S]), ALU.add).then_inc(s_zT, 1)
                if not last:
                    for n in range(PARTS):
                        split_lo(i, last, 2, n)
                dve.wait_ge(s_blk, i * U * 2 + UL * 2)
                dve.wait_ge(s_job, banks.done(i, last, ("Q1", 0)))
                bank = job_ps[banks.slot(i, last, ("Q1", 0))][:, 0:KT * S].rearrange("p (k s) -> p k s", k=KT)
                nc.vector.tensor_scalar(q_hi[:, :, :], bank, SCALE, None, ALU.mult).then_inc(s_q, 1)
                dve.wait_ge(s_q, i * 3 + 3)
                nc.vector.scalar_tensor_tensor(out=q_lo[:, :, :], in0=bank, scalar=SCALE, in1=q_hi[:, :, :].bitcast(F32),
                                               op0=ALU.mult, op1=ALU.subtract).then_inc(s_free_dve, 1)
                take_max(i, UL, 0, N_UNIT)

            def finish(i, last):
                dve.wait_ge(s_job, banks.done(i, last, ("out", 1)))
                nc.vector.tensor_tensor(resid[:, :], job_ps[banks.slot(i, last, ("out", 1))][0:S, :], resid[:, :], ALU.add).then_inc(s_free_dve, 1)

            with dve.Fori(0, B - 1) as i:
                batch(i, False)
            batch(B - 1, True)

        @block.gpsimd
        def _(pool):
            def spread_queries(i, last, u):
                ct = u % UL
                shape = [P, HU, S]
                m = hmask[:, :].unsqueeze(2).to_broadcast(shape)
                if UL <= u < U:
                    pool.wait_ge(s_free_dve, banks.freed(i, last, ("Q1", 0)))
                else:
                    pool.wait_ge(s_q, i * 3 + (2 if u < UL else 5))
                if u >= 2:
                    pool.wait_ge(s_score, i * N_SC + (u - 1) * J)
                nc.gpsimd.tensor_tensor(blk_hi[:, par(u), :, :], q_hi[:, ct, :].bitcast(F32).unsqueeze(1).to_broadcast(shape), m, ALU.mult).then_inc(s_blk, 1)
                nc.gpsimd.tensor_tensor(blk_lo[:, par(u), :, :], q_lo[:, ct, :].unsqueeze(1).to_broadcast(shape), m, ALU.mult).then_inc(s_blk, 1)

            def spread_max(i, u):
                pool.wait_ge(s_rowmax, i * U + (u + 1))
                shape = [PW, PAIRS, PW]
                nc.gpsimd.tensor_tensor(shift[:, par(u), :].rearrange("p (a c) -> p a c", a=PAIRS),
                                        ident_sb[:, :].unsqueeze(1).to_broadcast(shape),
                                        minus_max[:, par(u), :].unsqueeze(2).to_broadcast(shape), ALU.mult).then_inc(s_shift, 1)

            pool.wait_ge(s_consts, CONSTS)
            pool.wait_ge(s_fill, 3)
            spread_queries(0, False, 0)
            spread_max(0, 0)

            def batch(i, last):
                spread_queries(i, last, 1)
                pool.wait_ge(s_x, i * 16 + 16)
                nc.gpsimd.tensor_tensor(resid[:, :], resid[:, :], bo_row[:, :], ALU.add).then_inc(s_resid, 1)
                spread_max(i, 1)
                for u in range(1, UL - 1):
                    spread_queries(i, last, u + 1)
                    spread_max(i, u + 1)
                for n in range(2):
                    pool.wait_ge(s_var, i * 2 + (n + 1))
                    nc.gpsimd.tensor_tensor(rstd[:, n, :], vpe[:, n, :], minus_half[:, :], ALU.pow).then_inc(s_rstd, 1)
                spread_queries(i, last, UL)
                spread_max(i, UL)
                for u in range(UL, U):
                    if u + 1 < U or not last:
                        spread_queries(i, last, u + 1)
                        spread_max(i, u + 1)

            with pool.Fori(0, B - 1) as i:
                batch(i, False)
            batch(B - 1, True)


def kernel(x, ctx_4096, mask_BxS2_ik0, mask_BxS2_bf1, L0_xattn_Wq, L0_xattn_bq, L0_xattn_Wk, L0_xattn_bk,
           L0_xattn_Wv, L0_xattn_bv, L0_xattn_Wo, L0_xattn_bo, L0_xattn_ln_g, L0_xattn_ln_b,
           L1_xattn_Wq, L1_xattn_Wout, L1_xattn_ln_gamma, L1_xattn_ln_beta):
    import numpy as np
    import concourse.bacc as bacc
    from concourse.bass_utils import run_bass_kernel_spmd

    x, ctx = np.asarray(x), np.asarray(ctx_4096)
    mask0 = np.asarray(mask_BxS2_ik0)
    mask1 = np.asarray(mask_BxS2_bf1).view(np.uint8)
    by_channel = lambda v: np.ascontiguousarray(np.asarray(v).reshape(KT, P).T)
    turned = lambda w: np.ascontiguousarray(np.asarray(w).T)
    positions = lambda m: np.ascontiguousarray(m.reshape(B, TP, J).transpose(1, 0, 2).reshape(TP, B * J))
    heads = np.arange(P)[:, None] // HD == np.arange(HU)[None, :]
    halves = (np.arange(P)[:, None] // HD) % 2 == np.arange(2)[None, :]
    arrays = {
        "x": x,
        "xT": turned(x.reshape(B * S, H)),
        "ctx": ctx,
        "ctxT": np.ascontiguousarray(ctx.reshape(B, TP, J, H).transpose(0, 3, 2, 1).reshape(B, H, T)),
        "mask0": positions(mask0), "mask1": positions(mask1),
        "mask0T": turned(positions(mask0)), "mask1T": turned(positions(mask1)),
        "Wq0T": turned(L0_xattn_Wq), "bq": by_channel(L0_xattn_bq),
        "Wk0T": turned(L0_xattn_Wk), "bk": by_channel(L0_xattn_bk),
        "Wv0T": turned(L0_xattn_Wv), "bv": by_channel(L0_xattn_bv),
        "Wo0T": turned(L0_xattn_Wo), "bo": np.asarray(L0_xattn_bo),
        "ln_g": np.asarray(L0_xattn_ln_g), "ln_b": np.asarray(L0_xattn_ln_b),
        "Wq1T": turned(L1_xattn_Wq), "Wo1T": turned(L1_xattn_Wout),
        "gamma": by_channel(L1_xattn_ln_gamma), "beta": by_channel(L1_xattn_ln_beta),
        "ident": np.eye(PW, dtype=np.float32),
        "headmask": heads.astype(np.float32), "halves": halves.astype(np.float32),
        "quarters": np.repeat(np.arange(P)[:, None] % CG == 0, CG, 1).astype(np.float32),
    }
    nc = bacc.Bacc("TRN2", target_bir_lowering=False, num_devices=1)
    args = {n: nc.dram_tensor(f"in_{n}_dram", a.shape, mybir.dt.from_np(a.dtype), kind="ExternalInput").ap() for n, a in arrays.items()}
    args["out"] = nc.dram_tensor("out_dram", (B, S, H), F32, kind="ExternalOutput").ap()
    cross_attention(nc, **args)
    r = run_bass_kernel_spmd(nc, [{f"in_{n}_dram": a for n, a in arrays.items()}], core_ids=[0])
    return r.results[0]["out_dram"]
```

```python
from contextlib import ExitStack

import concourse.bass as bass
from concourse import mybir

F32 = mybir.dt.float32
F32R = mybir.dt.float32r
BF16 = mybir.dt.bfloat16
I32 = mybir.dt.int32
U8 = mybir.dt.uint8
ALU = mybir.AluOpType
ACT = mybir.ActivationFunctionType

B, S, T, H = 8, 56, 1500, 512
HD = 16
P = 128
KT = H // P
HU = P // HD
J = 12
TP = T // J
NC = 3
CW = T // NC
JC = J // NC
W = HU * S
PAIRS = 4
PW = 2 * S
CG = 32
UL = KT
U = 2 * UL
RING = 4
SC = 3
EPS = 1e-5
MASKED = -3e38
FLOOR = -1e37
SCALE = HD ** -0.5
VB = H // 32

K_AT = {0: 0, 1: 1, 2: 2}
KEY_MAX = {1: (0, 1, 1, 1), 2: (1, 1, 1, 1)}
MAX_AT = ({3: 1, 4: 1, 5: 1, 6: 1, 7: 1},
          {2: 1, 3: 2, 4: 2, 5: 1, 6: 2, 7: 2, 8: 2})
SHIFT_AT = (7, 8)
DIVIDE_AT = (8, 9, 10)
SPLIT_OF = {3: 0, 4: 3, 5: 4, 6: 5, 7: 6}
SPLIT_AT = ({1: 0, 2: 1, 6: 2, 9: 3},
            {1: 0, 2: 1, 3: 2, 4: 3})
Q_AT = 5
PARTS = 4
PT = T // PARTS
JV = J // PARTS
TENSOR_TILES = (4, 10)
TAIL = 2
LAG = 2
SUM_AT = 1
BETWEEN_LAYERS = [("V", 0), ("sum", 3), ("V", 1), ("out", 0), ("V", 2), ("V", 3), ("V", 4), ("z", 0), ("V", 5), ("Q1", 0),
                  ("V", 6, (0, 0, 1, 2)), ("V", 7, (1, 2, 2, 2)), ("V", 8, (2, 0, 0, 0))]
BETWEEN_BATCHES = [("V", 9), ("sum", 7), ("K", 0), ("out", 1), ("K", 1, (1, 1, 1, 1)), ("K", 2, (0, 1, 2, 1)),
                   ("V", 10, (0, 1, 2, 1)), ("V", 11)]
START = [("V", j) for j in range(J - 2)] + [("K", 0)] + BETWEEN_BATCHES[4:]


class Banks:

    def __init__(self):
        job = lambda kind, n: (kind, n, "act" if kind in ("V", "Q", "row") else "dve")
        key = lambda ct: [job("K", ct * NC + c) for c in range(NC)]
        between = lambda plan: [job(*x[:2]) for x in plan]
        self.pro = [job("Q", ct) for ct in range(KT)] + between(START)
        layer0 = [job("row", 0)] + key(1)
        for u in range(1, UL):
            keys = key(u + 1) if u + 1 < UL else []
            layer0 += [job("row", u)] + keys[:1] + [job("sum", u - 1)] + keys[1:]
        layer1 = [job("row", UL)] + [x for u in range(UL + 1, U) for x in (job("row", u), job("sum", u - 1))]
        self.loop = layer0 + between(BETWEEN_LAYERS) + layer1 + between(BETWEEN_BATCHES)
        skip = lambda js: [x for x in js if x[0] != "V"]
        self.tail = layer0 + skip(between(BETWEEN_LAYERS)) + layer1 + [job("sum", U - 1), job("out", 1)]
        assert len(self.loop) % 2 == 0 and self.pro[-2:] == self.loop[-2:]

    def jobs(self, i, last):
        return self.pro if i is None else self.tail if last else self.loop

    def slot(self, i, last, key):
        at = [x[:2] for x in self.jobs(i, last)].index(key)
        base = 0 if i is None else len(self.pro)
        assert len(self.loop) % 2 == 0
        return (base + at) % 2

    def done(self, i, last, key):
        at = [x[:2] for x in self.jobs(i, last)].index(key) + 1
        return at if i is None else i * len(self.loop) + (len(self.pro) + at)

    def done_ahead(self, i):
        return i * len(self.loop) + len(self.pro)

    def freed(self, i, last, key):
        jobs = self.jobs(i, last)
        at = [x[:2] for x in jobs].index(key)
        count = lambda js: sum(x[2] == jobs[at][2] for x in js)
        here = count(jobs[: at + 1])
        return here if i is None else i * count(self.loop) + (count(self.pro) + here)

    def freed_ahead(self, i):
        count = lambda js: sum(x[2] == "dve" for x in js)
        return i * count(self.loop) + count(self.pro)

    def freed_by_act(self, i):
        count = lambda js: sum(x[2] == "act" for x in js)
        return i * count(self.loop) + count(self.pro)

    def before(self, i, last, key):
        jobs = self.jobs(i, last)
        at = [x[:2] for x in jobs].index(key) - 2
        count = lambda js, who: sum(x[2] == who for x in js)
        if i is None:
            if at < 0:
                return None
            who = jobs[at][2]
            return who, count(jobs[: at + 1], who)
        if at >= 0:
            who = jobs[at][2]
            return who, i * count(self.loop, who) + (count(self.pro, who) + count(jobs[: at + 1], who))
        who = self.loop[at][2]
        return who, i * count(self.loop, who) + (count(self.pro, who) - count(self.loop[len(self.loop) + at + 1:], who))


class Steps:

    def __init__(self, eng, sem, base, i, per):
        self.eng, self.sem, self.n, self.i, self.per = eng, sem, base, i, per

    def value(self):
        return self.n if self.i is None else self.i * self.per + self.n

    def inc(self, ins):
        self.n += 1
        ins.then_inc(self.sem, 1)

    def wait(self):
        self.eng.wait_ge(self.sem, self.value())


def cross_attention(nc, x, xT, ctx, ctxT, mask0, mask1, mask0T, mask1T,
                    Wq0T, bq, Wk0T, bk, Wv0T, bv, Wo0T, bo, ln_g, ln_b,
                    Wq1T, Wo1T, gamma, beta, ident, headmask, halves, out):
    banks = Banks()
    stack = ExitStack()
    with stack:
        def sb(name, shape, dt=F32):
            return stack.enter_context(nc.sbuf_tensor(name, shape, dt))

        def psum(name, shape, dt=F32):
            return stack.enter_context(nc.psum_tensor(name, shape, dt))

        def sem(name):
            return stack.enter_context(nc.semaphore(name))

        vals = sb("vals", [P, 2 * J * VB + 1, 32])
        ONES = 2 * J * VB
        e_flat = vals[:, 0:J * VB, :].rearrange("p n c -> p (n c)")
        e_raw = e_flat[:, 0:KT * T].rearrange("p (k t) -> p k t", k=KT)
        a_flat = vals[:, J * VB:2 * J * VB, :].rearrange("p n c -> p (n c)")
        xt_hi = sb("xt_hi", [P, KT, T], F32R)
        xt_lo = sb("xt_lo", [P, KT, T], F32R)
        key_hi = sb("key_hi", [P, 2, T], F32R)
        key_lo = sb("key_lo", [P, 2, T], F32R)
        wk_hi = sb("wk_hi", [P, KT, H], F32R)
        wk_lo = sb("wk_lo", [P, KT, H], F32R)
        wv_hi = sb("wv_hi", [P, KT, H], F32R)
        wv_lo = sb("wv_lo", [P, KT, H], F32R)
        wq1 = sb("wq1", [P, KT, H])
        wo = sb("wo", [P, KT, H])
        raw = sb("raw", [P, T])
        q_hi = sb("q_hi", [P, KT, S], F32R)
        q_lo = sb("q_lo", [P, KT, S])
        blk_hi = sb("blk_hi", [P, 2, HU, S], F32R)
        blk_lo = sb("blk_lo", [P, 2, HU, S], F32R)
        shift = sb("shift", [PW, W], F32R)
        shift_row = sb("shift_row", [P, W])
        chunk_max = sb("chunk_max", [PW, 2, PAIRS, NC])
        minus_max = sb("minus_max", [PW, 2, PAIRS])
        bias_row = sb("bias_row", [PW, T], BF16)
        bias_col = sb("bias_col", [TP, 2, B, J])
        bias_now = sb("bias_now", [TP, 2, J])
        probs = sb("probs", [P, RING * W])
        norm = probs[0:S, 0:H]
        resid = sb("resid", [S, H])
        g_row = sb("g_row", [S, H])
        b_row = sb("b_row", [S, H])
        bo_row = sb("bo_row", [S, H])
        acc = sb("acc", [P, W])
        numer = sb("numer", [P, PW])
        recip = sb("recip", [P, PW])
        half0 = numer[:, 0:S]
        attn = sb("attn", [P, KT, S])
        zT = acc[:, 0:KT * S].rearrange("p (k s) -> p k s", k=KT)
        cols = sb("cols", [P, 5, KT])
        bq_raw = sb("bq_raw", [P, KT])
        stats = sb("stats", [S, 6])
        mv = sb("mv", [S, 2, 2])
        rstd = sb("rstd", [S, 2, 1])
        vpe = sb("vpe", [S, 2, 1])
        minus_half = sb("minus_half", [S, 1])
        ident_sb = sb("ident_sb", [PW, PW])
        ones_r = sb("ones_r", [PW, 1], F32R)
        hmask = sb("hmask", [P, HU])
        hsel = sb("hsel", [P, 2])

        sc_ps = [psum(f"sc_ps{n}", [P, 512]) for n in range(SC)]
        max_ps = [psum(f"max_ps{n}", [P, 512]) for n in range(2)]
        pv_ps = psum("pv_ps", [P, 512])
        job_ps = [psum(f"job_ps{n}", [P, 512]) for n in range(2)]

        q0_dram = nc.dram_tensor("queries0", [P, KT, B * S], F32, kind="Internal").ap()
        bias_dram = nc.dram_tensor("bias_rows", [2, B * J, TP], BF16, kind="Internal").ap()

        s_consts = sem("s_consts")
        s_q0w = sem("s_q0w")
        s_wv = sem("s_wv")
        s_wk = sem("s_wk")
        s_rows = sem("s_rows")
        s_wo = sem("s_wo")
        s_first = [sem(f"s_first{k}") for k in range(KT)]
        s_raw = sem("s_raw")
        s_ctx = sem("s_ctx")
        s_x = sem("s_x")
        s_maskin = sem("s_maskin")
        s_biasout = sem("s_biasout")
        s_bias = sem("s_bias")
        s_out = sem("s_out")
        s_fill = sem("s_fill")
        s_wv_split = sem("s_wv_split")
        s_wk_hi = sem("s_wk_hi")
        s_wk_lo = sem("s_wk_lo")
        s_bq = sem("s_bq")
        s_mask = sem("s_mask")
        s_job = sem("s_job")
        s_free_act = sem("s_free_act")
        s_free_dve = sem("s_free_dve")
        s_key_hi = sem("s_key_hi")
        s_split_hi = sem("s_split_hi")
        s_split_lo = sem("s_split_lo")
        s_q0out = sem("s_q0out")
        s_q0in = sem("s_q0in")
        s_q = sem("s_q")
        s_blk = sem("s_blk")
        s_max = sem("s_max")
        s_red = sem("s_red")
        s_rowmax = sem("s_rowmax")
        s_shift = sem("s_shift")
        s_score = sem("s_score")
        s_sub = sem("s_sub")
        s_exp = sem("s_exp")
        s_pv = sem("s_pv")
        s_acc = sem("s_acc")
        s_numer = sem("s_numer")
        s_attn = sem("s_attn")
        s_dve = sem("s_dve")
        s_bnow = sem("s_bnow")
        s_passed = sem("s_passed")
        s_resid = sem("s_resid")
        s_var = sem("s_var")
        s_rstd = sem("s_rstd")
        s_norm = sem("s_norm")
        s_zT = sem("s_zT")

        N_SC = U * J
        N_ACC = J - 1 - TAIL
        N_SUB = UL * sum(J - x for x in TENSOR_TILES)
        N_ACCS = U * N_ACC
        N_UNIT = PAIRS * NC
        N_RED = U * N_UNIT
        L_RED = UL * N_UNIT
        DVE_STEPS = U * 2 + 6
        CONSTS = 8 * 16

        q0_all = probs[:, 0:KT * B * S].rearrange("p (k n) -> p k n", k=KT)
        raw_wk, raw_wv, raw_wq0 = (a_flat[:, n * KT * H:(n + 1) * KT * H].rearrange("p (k n) -> p k n", k=KT) for n in range(3))
        xT_sb = wo[:, :, :].rearrange("p k n -> p (k n)")[:, 0:KT * B * S].rearrange("p (k n) -> p k n", k=KT)
        m0 = B * J
        mask_cols = [raw[0:TP, 0:m0].bitcast(I32), raw[0:TP, 240:240 + m0 // 4].bitcast(U8)]
        mask_rows = [raw[0:m0, 100:100 + TP].bitcast(I32), raw[0:m0, 280:280 + 32].bitcast(U8)[:, 0:TP]]
        bias_bf = raw[0:m0, 600:600 + TP].bitcast(BF16).rearrange("p (l t) -> p l t", l=2)
        L0_KEYS = UL * NC

        block = stack.enter_context(nc.Block())


        LOADS = 2 * PARTS
        SPLITS = LOADS * PARTS

        def part_of(n, step):
            t = slice(step * PT, (step + 1) * PT)
            if n < PARTS:
                return raw[:, t], key_hi[:, n % 2, t], key_lo[:, n % 2, t]
            return raw[:, t], xt_hi[:, n - PARTS, t], xt_lo[:, n - PARTS, t]

        def place_free(eng, i, last, n):
            if n < 2:
                eng.wait_ge(s_score, i * N_SC + (n + 3) * J)
            elif n < PARTS:
                eng.wait_ge(s_job, banks.done(i, last, ("V", JV * (n - 1) - 1)))
            else:
                eng.wait_ge(s_score, i * N_SC + (UL + 1 + n - PARTS) * J)

        def par(u):
            return u % 2

        def subtracts(n):
            return n % J >= TENSOR_TILES[n // J // UL]

        def first_product(u, j):
            behind_keys = sum(sum(KEY_MAX[x]) for x in KEY_MAX if x < j) if u < UL else 0
            return behind_keys + sum(n for x, n in MAX_AT[u // UL].items() if x < j)

        def sub_count(n):
            return sum(subtracts(x) for x in range(n + 1))

        def split_at(u):
            return SPLIT_AT[u % UL == UL - 1]

        def acc_count(n):
            return n // J * N_ACC + max(n % J, 1)

        @block.sync
        def _(sp):
            by_rows = lambda w: w.rearrange("(k p) n -> p k n", p=P)
            sp.dma_start(raw_wq0, by_rows(Wq0T)).then_inc(s_q0w, 16)
            sp.dma_start(xT_sb, by_rows(xT)).then_inc(s_q0w, 16)
            for src, dst in ((mask0, mask_cols[0]), (mask1, mask_cols[1]), (mask0T, mask_rows[0]), (mask1T, mask_rows[1])):
                sp.dma_start(dst, src).then_inc(s_maskin, 16)
            for dst, src in ((bq_raw[:, :], bq), (cols[:, 1, :], bk), (cols[:, 2, :], bv), (cols[:, 3, :], gamma),
                             (cols[:, 4, :], beta), (ident_sb[:, :], ident), (hmask[:, :], headmask), (hsel[:, :], halves)):
                sp.dma_start(dst, src).then_inc(s_consts, 16)
            for k in range(KT):
                sp.dma_start(e_raw[:, k, :], ctxT[0, k * P:(k + 1) * P, :]).then_inc(s_first[k], 16)
                if k == 1:
                    sp.dma_start(raw_wv, by_rows(Wv0T)).then_inc(s_wv, 16)
            sp.dma_start(raw_wk, by_rows(Wk0T)).then_inc(s_wk, 16)
            sp.wait_ge(s_mask, 4)
            for layer in range(2):
                sp.dma_start(bias_dram[layer], bias_bf[:, layer, :]).then_inc(s_biasout, 16)
            for dst, src in ((g_row, ln_g), (b_row, ln_b), (bo_row, bo)):
                sp.dma_start(dst[:, :], src.partition_broadcast(S)).then_inc(s_rows, 16)
            sp.dma_start(wq1[:, :, :], by_rows(Wq1T)).then_inc(s_rows, 16)
            sp.wait_ge(s_biasout, 32)
            sp.dma_start(bias_row[:, :], bias_dram[0, 0:J, :].rearrange("j p -> (j p)").partition_broadcast(PW)).then_inc(s_bias, 16)
            sp.wait_ge(s_job, banks.done(None, False, ("Q", KT - 1)))
            sp.dma_start(wo[:, :, :], Wo0T.rearrange("(k p) n -> p k n", p=P)).then_inc(s_wo, 16)
            sp.dma_start(resid[:, :], x[0]).then_inc(s_x, 16)
            sp.wait_ge(s_free_act, KT)
            sp.dma_start(q0_dram, q0_all).then_inc(s_q0out, 16)
            sp.wait_ge(s_q0out, 16)
            sp.dma_start(q_lo[:, :, :], q0_dram[:, :, 0:S]).then_inc(s_q0in, 16)
            sp.wait_ge(s_wv_split, 2)
            sp.wait_ge(s_wk_lo, 1)
            sp.dma_start(a_flat[0:TP, :], ctx[0].rearrange("(p j) d -> p (j d)", j=J)).then_inc(s_ctx, 16)

            def load_part(i, n):
                sp.wait_ge(s_split_lo, i * SPLITS + (n + PARTS) * PARTS)
                if n < PARTS:
                    src = ctxT[i + 1, :, n * PT:(n + 1) * PT].rearrange("(k p) t -> p k t", p=P)
                    sp.dma_start(raw[:, :].rearrange("p (k t) -> p k t", k=KT), src).then_inc(s_raw, 16)
                else:
                    ct = n - PARTS
                    sp.dma_start(raw[:, :], ctxT[i + 1, ct * P:(ct + 1) * P, :]).then_inc(s_raw, 16)

            def batch(i, last):
                if not last:
                    load_part(i, 0)
                sp.wait_ge(s_red, i * N_RED + L_RED)
                sp.dma_start(bias_row[:, :], bias_dram[1, bass.ts(i, J), :].rearrange("j p -> (j p)").partition_broadcast(PW)).then_inc(s_bias, 16)
                if not last:
                    load_part(i, 1)
                    load_part(i, 2)
                sp.wait_ge(s_job, banks.done(i, last, ("out", 0)))
                sp.dma_start(wo[:, :, :], Wo1T.rearrange("(k p) n -> p k n", p=P)).then_inc(s_wo, 16)
                if not last:
                    load_part(i, 3)
                    load_part(i, 4)
                    load_part(i, 5)
                    load_part(i, 6)
                    sp.wait_ge(s_red, i * N_RED + N_RED)
                    sp.dma_start(bias_row[:, :], bias_dram[0, bass.ts(i + 1, J), :].rearrange("j p -> (j p)").partition_broadcast(PW)).then_inc(s_bias, 16)
                    sp.wait_ge(s_blk, (i * U + U) * 2)
                    sp.dma_start(q_lo[:, :, :], q0_dram[:, :, bass.ts(i + 1, S)]).then_inc(s_q0in, 16)
                    load_part(i, 7)
                    sp.wait_ge(s_pv, (i + 1) * N_SC)
                    sp.dma_start(a_flat[0:TP, :], ctx[i + 1].rearrange("(p j) d -> p (j d)", j=J)).then_inc(s_ctx, 16)
                sp.wait_ge(s_free_dve, banks.freed(i, last, ("out", 1)))
                sp.dma_start(out[i], resid[:, :]).then_inc(s_out, 16)
                if not last:
                    sp.dma_start(wo[:, :, :], Wo0T.rearrange("(k p) n -> p k n", p=P)).then_inc(s_wo, 16)
                    sp.wait_ge(s_out, i * 16 + 16)
                    sp.dma_start(resid[:, :], x[i + 1]).then_inc(s_x, 16)

            with sp.Fori(0, B - 1) as i:
                batch(i, False)
            batch(B - 1, True)
            sp.wait_ge(s_out, B * 16)

        @block.tensor
        def _(pe):
            def take_bank(i, last, key):
                if (need := banks.before(i, last, key)) is not None:
                    pe.wait_ge(s_free_act if need[0] == "act" else s_free_dve, need[1])
                return job_ps[banks.slot(i, last, key)]

            def split_product(dst, terms, more=False):
                for n, (a, b) in enumerate(terms):
                    mm = pe.matmul(dst, a, b, start=n == 0, stop=n == len(terms) - 1 and not more)
                return mm

            def project_key(i, last, n, between=lambda k: None):
                if i is None and n == 0:
                    pe.wait_ge(s_wk_hi, 1)
                    pe.wait_ge(s_wk_lo, 1)
                ct, c = divmod(n, NC)
                bank = take_bank(i, last, ("K", n))
                w = slice(ct * P, (ct + 1) * P)
                t = slice(c * CW, (c + 1) * CW)
                for k in range(KT):
                    if i is not None and ct == 0 and c == 0:
                        pe.wait_ge(s_split_lo, i * SPLITS + (PARTS + PARTS + k + 1) * PARTS)
                    for m, (a, b) in enumerate(((wk_hi[:, k, w], xt_hi[:, k, t]), (wk_hi[:, k, w], xt_lo[:, k, t]),
                                                (wk_lo[:, k, w], xt_hi[:, k, t]))):
                        mm = pe.matmul(bank[:, 0:CW], a, b, start=k == 0 and m == 0, stop=k == KT - 1 and m == 2)
                    if k == KT - 1:
                        mm.then_inc(s_job, 1)
                    between(k)

            def project_value(i, last, j, between=lambda k: None):
                bank = take_bank(i, last, ("V", j))
                if i is None:
                    hi, lo, t = xt_hi, xt_lo, slice(j * TP, (j + 1) * TP)
                else:
                    n = j // JV
                    pe.wait_ge(s_split_lo, i * SPLITS + (n + 1 + PARTS) * PARTS)
                    hi, lo = (x[:, n % 2, :].rearrange("p (k t) -> p k t", k=KT) for x in (key_hi, key_lo))
                    t = slice((j % JV) * TP, (j % JV + 1) * TP)
                for k in range(KT):
                    if i is None and j == 0:
                        pe.wait_ge(s_split_lo, (k + 1) * PARTS)
                    for m, (a, b) in enumerate(((hi[:, k, t], wv_hi[:, k, :]), (hi[:, k, t], wv_lo[:, k, :]), (lo[:, k, t], wv_hi[:, k, :]))):
                        mm = pe.matmul(bank[0:TP, :], a, b, start=k == 0 and m == 0, stop=k == KT - 1 and m == 2)
                    if k == KT - 1:
                        mm.then_inc(s_job, 1)
                    between(k)

            def max_rows(i, u, first, count):
                for n in range(first, first + count):
                    c, p = divmod(n, PAIRS)
                    if n == 0:
                        pe.wait_ge(s_blk, (i * U + u) * 2 + 1)
                    if p == 0 and u % U < UL:
                        pe.wait_ge(s_key_hi, i * L0_KEYS + ((u // U) * L0_KEYS + (u % U * NC + c + 1)))
                    keys = key_hi[:, par(u), :] if u % U < UL else xt_hi[:, u % U - UL, :]
                    q = blk_hi[:, par(u), 2 * p:2 * p + 2, :].rearrange("p h s -> p (h s)")
                    m = u * N_UNIT + n
                    if not (isinstance(i, int) and i == 0 and m < 2):
                        pe.wait_ge(s_red, i * N_RED + (m - 1))
                    pe.matmul(max_ps[m % 2][0:PW, 0:CW], q, keys[:, c * CW:(c + 1) * CW], start=True, stop=True).then_inc(s_max, 1)

            def score(i, last, u, j):
                n = u * J + j
                if n >= SC:
                    pe.wait_ge(s_exp, i * N_SC + (n + 1 - SC))
                if j == 0:
                    pe.wait_ge(s_shift, i * U + (u + 1))
                    if u < UL:
                        pe.wait_ge(s_free_dve, banks.freed(i, last, ("K", u * NC + NC - 1)) if u else banks.freed_ahead(i))
                t = slice(j * TP, (j + 1) * TP)
                if u < UL:
                    hi, lo = key_hi[:, par(u), t], key_lo[:, par(u), t]
                else:
                    hi, lo = xt_hi[:, u - UL, t], xt_lo[:, u - UL, t]
                qh = blk_hi[:, par(u), :, :].rearrange("p h s -> p (h s)")
                ql = blk_lo[:, par(u), :, :].rearrange("p h s -> p (h s)")
                terms = [(hi, qh), (hi, ql), (lo, qh)]
                if not subtracts(n):
                    terms.append((ones_r[:, :].to_broadcast([PW, TP]), shift[:, :]))
                split_product(sc_ps[n % SC][0:TP, 0:W], terms).then_inc(s_score, 1)

            def maximum_row(i, last, u):
                bank = take_bank(i, last, ("row", u))
                pe.matmul(bank[0:TP, 0:W], ones_r[:, :].to_broadcast([PW, TP]), shift[:, :], start=True, stop=True).then_inc(s_job, 1)

            def weigh(i, u, j):
                n = u * J + j
                pe.wait_ge(s_exp, i * N_SC + (n + 1))
                if j == 0:
                    if u:
                        pe.wait_ge(s_numer, i * U + u)
                    if u == 0:
                        pe.wait_ge(s_free_act, banks.freed_by_act(i))
                    if u == UL:
                        pe.wait_ge(s_ctx, i * 16 + 16)
                ring = (n % RING) * W
                for p in range(PAIRS):
                    v0 = (u % UL) * PAIRS + p + (0 if u < UL else J * VB) + j * VB
                    mm = pe.matmul(pv_ps[CG * p:CG * p + CG, 0:PW], vals[0:TP, v0, :], probs[0:TP, ring + p * PW:ring + (p + 1) * PW],
                                   start=j == 0, stop=j == J - 1, skip_group_check=True, tile_position=(0, CG * p))
                mm.then_inc(s_pv, 1)

            def total(i, last, u):
                pe.wait_ge(s_exp, i * N_SC + (u + 1) * J)
                bank = take_bank(i, last, ("sum", u))
                pe.wait_ge(s_acc, (i * U + (u + 1)) * N_ACC)
                tail = [probs[:, (u * J + J - TAIL + n) % RING * W:][:, 0:W] for n in range(TAIL)]
                for n, x in enumerate([acc] + tail):
                    for p in range(PAIRS):
                        mm = pe.matmul(bank[CG * p:CG * p + CG, 0:PW], vals[0:TP, ONES, :], x[0:TP, p * PW:(p + 1) * PW],
                                       start=n == 0, stop=n == TAIL, skip_group_check=True, tile_position=(0, CG * p))
                mm.then_inc(s_job, 1)

            def output(i, last, layer):
                bank = take_bank(i, last, ("out", layer))
                pe.wait_ge(s_attn, i * U + (layer + 1) * UL)
                pe.wait_ge(s_wo, i * 32 + 16 * (layer + 1))
                for k in range(KT):
                    mm = pe.matmul(bank[0:S, :], attn[:, k, :], wo[:, k, :], start=k == 0, stop=k == KT - 1)
                mm.then_inc(s_job, 1)

            def main_pass(i, last, u):
                for j in range(J):
                    score(i, last, u, j)
                    at = MAX_AT[u // UL] if u % UL != UL - 1 else {}
                    first = first_product(u, j)
                    ahead = j > 1 and at.get(j, 0) == 2
                    if ahead:
                        max_rows(i, u + 1, first, 1)
                    if u % UL or j >= LAG:
                        weigh(i, u - (j < LAG), (j - LAG) % J)
                    if j == 0:
                        maximum_row(i, last, u)
                    if j == SUM_AT and u % UL:
                        total(i, last, u - 1)
                    if j in at:
                        max_rows(i, u + 1, first + ahead, at[j] - ahead)
                    if j in K_AT and u < UL - 1:
                        done = first

                        def products(k):
                            nonlocal done
                            if j in KEY_MAX:
                                max_rows(i, u + 1, done, KEY_MAX[j][k])
                                done += KEY_MAX[j][k]

                        project_key(i, last, (u + 1) * NC + K_AT[j], products)

            def to_layer1(i, last):
                pe.wait_ge(s_consts, CONSTS)
                bank = take_bank(i, last, ("z", 0))
                pe.wait_ge(s_norm, i + 1)
                pe.sem_inc(s_passed, 1)
                for k in range(KT):
                    mm = pe.transpose(bank[:, k * S:(k + 1) * S], norm[:, k * P:(k + 1) * P], ident_sb[0:S, 0:S])
                mm.then_inc(s_job, 1)

            def queries1(i, last):
                bank = take_bank(i, last, ("Q1", 0))
                pe.wait_ge(s_zT, i + 1)
                for ct in range(KT):
                    for k in range(KT):
                        mm = pe.matmul(bank[:, ct * S:(ct + 1) * S], wq1[:, k, ct * P:(ct + 1) * P], zT[:, k, :],
                                       start=k == 0, stop=k == KT - 1)
                mm.then_inc(s_job, 1)

            def between(i, last, plan, u):
                done = 0
                for x in plan:
                    def products(k):
                        nonlocal done
                        if i is not None and x is plan[0] and k < LAG:
                            weigh(i, u - 1, J - LAG + k)
                        if len(x) > 2:
                            max_rows(0 if i is None else i, u, done, x[2][k])
                            done += x[2][k]

                    if x[0] == "V" and not last:
                        project_value(i, last, x[1], products)
                    elif x[0] == "V":
                        for k in range(KT):
                            products(k)
                    elif x[0] == "K":
                        project_key(i, last, x[1], products)
                    elif x[0] == "sum":
                        total(i, last, x[1])
                    elif x[0] == "out":
                        output(i, last, x[1])
                    elif x[0] == "z":
                        to_layer1(i, last)
                    else:
                        queries1(i, last)

            pe.wait_ge(s_q0w, 32)
            for ct in range(KT):
                bank = take_bank(None, False, ("Q", ct))
                for k in range(KT):
                    mm = pe.matmul(bank[:, 0:B * S], raw_wq0[:, k, ct * P:(ct + 1) * P], xT_sb[:, k, :], start=k == 0, stop=k == KT - 1)
                mm.then_inc(s_job, 1)
            pe.wait_ge(s_fill, 3)
            pe.wait_ge(s_wv_split, 2)
            between(None, False, START, 0)
            pe.wait_ge(s_q0out, 16)
            pe.wait_ge(s_rows, 64)

            def batch(i, last):
                for u in range(UL):
                    main_pass(i, last, u)
                between(i, last, BETWEEN_LAYERS, UL)
                for u in range(UL, U):
                    main_pass(i, last, u)
                if last:
                    for k in range(LAG):
                        weigh(i, U - 1, J - LAG + k)
                    total(i, last, U - 1)
                    output(i, last, 1)
                else:
                    between(i, last, BETWEEN_BATCHES, U)

            with pe.Fori(0, B - 1) as i:
                batch(i, False)
            batch(B - 1, True)

        @block.scalar
        def _(act):
            def key_hi_part(i, last, n):
                ct, c = divmod(n, NC)
                act.wait_ge(s_job, banks.done(i, last, ("K", n)))
                nc.scalar.activation(key_hi[:, par(ct), c * CW:(c + 1) * CW], job_ps[banks.slot(i, last, ("K", n))][:, 0:CW],
                                     ACT.Identity, bias=cols[:, 1, ct:ct + 1]).then_inc(s_key_hi, 1)

            def split_hi(i, last, n, step):
                if step == 0:
                    act.wait_ge(s_raw, i * (16 * LOADS) + 16 * (n + 1))
                    place_free(act, i, last, n)
                src, hi, _ = part_of(n, step)
                nc.scalar.activation(hi, src, ACT.Copy).then_inc(s_split_hi, 1)

            def value_tile(i, last, j):
                act.wait_ge(s_job, banks.done(i, last, ("V", j)))
                nc.scalar.activation(e_flat[0:TP, j * H:(j + 1) * H], job_ps[banks.slot(i, last, ("V", j))][0:TP, :],
                                     ACT.Copy).then_inc(s_free_act, 1)

            def copy_numer(i, last, u):
                act.wait_ge(s_pv, i * N_SC + (u + 1) * J)
                if u:
                    act.wait_ge(s_attn, i * U + u)
                else:
                    act.wait_ge(s_free_dve, banks.freed_ahead(i))
                nc.scalar.activation(numer[:, :], pv_ps[:, 0:PW], ACT.Copy).then_inc(s_numer, 1)

            act.wait_ge(s_bq, 1)
            act.wait_ge(s_consts, CONSTS)
            for k in range(KT):
                act.wait_ge(s_job, banks.done(None, False, ("Q", k)))
                nc.scalar.activation(q0_all[:, k, :], job_ps[banks.slot(None, False, ("Q", k))][:, 0:B * S], ACT.Identity,
                                     bias=cols[:, 0, k:k + 1], scale=SCALE).then_inc(s_free_act, 1)
                act.wait_ge(s_first[k], 16)
                for n in range(PARTS):
                    t = slice(n * PT, (n + 1) * PT)
                    nc.scalar.activation(xt_hi[:, k, t], e_raw[:, k, t], ACT.Copy).then_inc(s_split_hi, 1)
            act.wait_ge(s_wk, 16)
            nc.scalar.activation(wk_hi[:, :, :], raw_wk, ACT.Copy).then_inc(s_wk_hi, 1)
            for j in range(J - 2):
                value_tile(None, False, j)
            for n in range(NC):
                key_hi_part(None, False, n)
            for j in (J - 2, J - 1):
                value_tile(None, False, j)

            def batch(i, last):
                for u in range(U):
                    layer = u // UL
                    if u % UL == 0:
                        act.wait_ge(s_bnow, i * 2 + (layer + 1))
                    for j in range(J):
                        n = u * J + j
                        if subtracts(n):
                            act.wait_ge(s_sub, i * N_SUB + sub_count(n))
                        else:
                            act.wait_ge(s_score, i * N_SC + (n + 1))
                        if n >= RING:
                            act.wait_ge(s_pv, i * N_SC + (n + 1 - RING))
                            if (n - RING) % J < J - TAIL:
                                act.wait_ge(s_acc, i * N_ACCS + acc_count(n - RING))
                            elif u != UL:
                                act.wait_ge(s_job, banks.done(i, last, ("sum", u - 1)))
                        if u == UL and j == 0:
                            act.wait_ge(s_job, banks.done(i, last, ("z", 0)))
                        nc.scalar.activation(probs[0:TP, (n % RING) * W:(n % RING + 1) * W], sc_ps[n % SC][0:TP, 0:W],
                                             ACT.Exp, bias=bias_now[:, layer, j:j + 1]).then_inc(s_exp, 1)
                        if j == 0:
                            act.wait_ge(s_job, banks.done(i, last, ("row", u)))
                            nc.scalar.activation(shift_row[0:TP, :], job_ps[banks.slot(i, last, ("row", u))][0:TP, 0:W],
                                                 ACT.Copy).then_inc(s_free_act, 1)
                        if j == LAG - 1 and u % UL:
                            copy_numer(i, last, u - 1)
                        if j in K_AT and u < UL - 1:
                            key_hi_part(i, last, (u + 1) * NC + K_AT[j])
                        if j in split_at(u) and u in SPLIT_OF and not last:
                            split_hi(i, last, SPLIT_OF[u], split_at(u)[j])
                    if u == UL - 1:
                        if not last:
                            for step in range(PARTS):
                                split_hi(i, last, 1, step)
                        copy_numer(i, last, u)
                        if not last:
                            for j in range(JV + 1):
                                value_tile(i, last, j)
                            for step in range(PARTS):
                                split_hi(i, last, 2, step)
                            for j in range(JV + 1, 3 * JV):
                                value_tile(i, last, j)
                if last:
                    copy_numer(i, last, U - 1)
                    return
                for step in range(PARTS):
                    split_hi(i, last, LOADS - 1, step)
                copy_numer(i, last, U - 1)
                value_tile(i, last, 3 * JV)
                for n in range(NC):
                    key_hi_part(i, last, n)
                for j in (J - 2, J - 1):
                    value_tile(i, last, j)

            with act.Fori(0, B - 1) as i:
                batch(i, False)
            batch(B - 1, True)

        @block.vector
        def _(dve):
            def key_lo_part(i, last, n):
                ct, c = divmod(n, NC)
                t = slice(c * CW, (c + 1) * CW)
                dve.wait_ge(s_key_hi, n + 1 if i is None else i * L0_KEYS + ((ct == 0) * L0_KEYS + n + 1))
                nc.vector.scalar_tensor_tensor(out=key_lo[:, par(ct), t], in0=job_ps[banks.slot(i, last, ("K", n))][:, 0:CW],
                                               scalar=cols[:, 1, ct:ct + 1], in1=key_hi[:, par(ct), t].bitcast(F32),
                                               op0=ALU.add, op1=ALU.subtract).then_inc(s_free_dve, 1)

            def split_lo(i, last, n, step):
                src, hi, lo = part_of(n, step)
                dve.wait_ge(s_split_hi, i * SPLITS + ((n + PARTS) * PARTS + step + 1))
                nc.vector.tensor_tensor(lo, src, hi.bitcast(F32), ALU.subtract).then_inc(s_split_lo, 1)

            def take_max(i, u, first, count):
                for n in range(first, first + count):
                    c, p = divmod(n, PAIRS)
                    m = u * N_UNIT + n
                    if n == 0:
                        if not (isinstance(i, int) and i == 0 and u == 0):
                            dve.wait_ge(s_shift, i * U + u)
                        dve.wait_ge(s_bias, i * 32 + 16 * (1 + u // UL))
                    dve.wait_ge(s_max, i * N_RED + (m + 1))
                    dve.sem_inc(s_passed, 1)
                    at = max_ps[m % 2][0:PW, 0:CW]
                    nc.vector.tensor_tensor_reduce(out=at, in0=at, in1=bias_row[:, c * CW:(c + 1) * CW], scale=1.0, scalar=FLOOR,
                                                   op0=ALU.add, op1=ALU.max, accum_out=chunk_max[:, par(u), p, c:c + 1]).then_inc(s_red, 1)
                    if n == N_UNIT - 1:
                        dve.wait_ge(s_red, i * N_RED + (m + 1))
                        nc.vector.tensor_reduce(minus_max[:, par(u), :], chunk_max[:, par(u), :, :], mybir.AxisListType.X, ALU.max, negate=True).then_inc(s_rowmax, 1)

            def subtract(i, last, u, j):
                n = u * J + j
                if j == TENSOR_TILES[u // UL]:
                    dve.wait_ge(s_free_act, banks.freed(i, last, ("row", u)))
                dve.wait_ge(s_score, i * N_SC + (n + 1))
                tile = sc_ps[n % SC][0:TP, 0:W]
                nc.vector.tensor_tensor(tile, tile, shift_row[0:TP, :], ALU.add).then_inc(s_sub, 1)

            def invert(i, last, u):
                if u:
                    dve.wait_ge(s_attn, i * U + u)
                dve.wait_ge(s_job, banks.done(i, last, ("sum", u)))
                nc.vector.reciprocal(recip[:, :], job_ps[banks.slot(i, last, ("sum", u))][:, 0:PW]).then_inc(s_free_dve, 1)

            def divide(i, last, u, step, parts=(0, 1, 2)):
                ct = u % UL
                if 0 in parts:
                    dve.wait_ge(s_free_dve, banks.freed(i, last, ("sum", u)))
                    dve.wait_ge(s_numer, i * U + (u + 1))
                    step.inc(nc.vector.tensor_tensor(recip[:, :], numer[:, :], recip[:, :], ALU.mult))
                if 1 in parts:
                    step.wait()
                    step.inc(nc.vector.tensor_scalar(half0[:, :], recip[:, 0:S], hsel[:, 0:1], cols[:, 2, ct:ct + 1] if u < UL else 0.0,
                                                     ALU.mult, ALU.add))
                if 2 in parts:
                    step.wait()
                    nc.vector.scalar_tensor_tensor(out=attn[:, ct, :], in0=recip[:, S:2 * S], scalar=hsel[:, 1:2], in1=half0[:, :],
                                                   op0=ALU.mult, op1=ALU.add).then_inc(s_attn, 1)

            def moments(i, n, src, step):
                step.inc(nc.vector.bn_stats(stats[:, :], src))
                step.wait()
                dve.sem_inc(s_passed, 1)
                step.inc(nc.vector.bn_aggr(mv[:, n, :], stats[:, :]))
                step.wait()
                nc.vector.tensor_scalar(vpe[:, n, :], mv[:, n, 1:2], EPS, None, ALU.add).then_inc(s_var, 1)

            nc.vector.memset(vals[:, ONES, :], 1.0).then_inc(s_fill, 1)
            nc.vector.memset(ones_r[:, :].bitcast(F32), 1.0).then_inc(s_fill, 1)
            nc.vector.memset(minus_half[:, :], -0.5).then_inc(s_fill, 1)
            dve.wait_ge(s_maskin, 64)
            for layer in range(2):
                nc.vector.tensor_scalar(bias_col[:, layer, :, :].rearrange("p b j -> p (b j)"), mask_cols[layer], 0.0, MASKED, ALU.is_equal, ALU.mult).then_inc(s_mask, 1)
                nc.vector.tensor_scalar(bias_bf[:, layer, :], mask_rows[layer], 0.0, MASKED, ALU.is_equal, ALU.mult).then_inc(s_mask, 1)
            dve.wait_ge(s_mask, 4)
            nc.vector.tensor_copy(bias_now[:, 0, :], bias_col[:, 0, 0, :]).then_inc(s_bnow, 1)
            dve.wait_ge(s_consts, CONSTS)
            nc.vector.tensor_scalar(cols[:, 0, :], bq_raw[:, :], SCALE, None, ALU.mult).then_inc(s_bq, 1)
            for k in range(KT):
                if k == 2:
                    dve.wait_ge(s_wv, 16)
                    nc.vector.tensor_copy(wv_hi[:, :, :], raw_wv).then_inc(s_wv_split, 1)
                    dve.wait_ge(s_wv_split, 1)
                    nc.vector.tensor_tensor(wv_lo[:, :, :], raw_wv, wv_hi[:, :, :].bitcast(F32), ALU.subtract).then_inc(s_wv_split, 1)
                for n in range(PARTS):
                    t = slice(n * PT, (n + 1) * PT)
                    dve.wait_ge(s_split_hi, k * PARTS + n + 1)
                    nc.vector.tensor_tensor(xt_lo[:, k, t], e_raw[:, k, t], xt_hi[:, k, t].bitcast(F32), ALU.subtract).then_inc(s_split_lo, 1)

            def queries0(i, count):
                dve.wait_ge(s_q0in, i * 16 + 16)
                nc.vector.tensor_copy(q_hi[:, :, :], q_lo[:, :, :]).then_inc(s_q, 1)
                dve.wait_ge(s_q, count + 1)
                nc.vector.tensor_tensor(q_lo[:, :, :], q_lo[:, :, :], q_hi[:, :, :].bitcast(F32), ALU.subtract).then_inc(s_q, 1)

            queries0(0, 0)
            for n in range(NC):
                key_lo_part(None, False, n)
                take_max(0, 0, n * PAIRS, PAIRS)
            dve.wait_ge(s_rows, 64)

            def batch(i, last):
                step = Steps(dve, s_dve, 0, i, DVE_STEPS)
                for u in range(U):
                    for j in range(J):
                        if u == U - 1 and j == Q_AT and not last:
                            queries0(i + 1, i * 3 + 3)
                        if j == SUM_AT and u % UL:
                            invert(i, last, u - 1)
                        if subtracts(u * J + j):
                            subtract(i, last, u, j)
                        at = MAX_AT[u // UL] if u % UL != UL - 1 else {}
                        if j in at:
                            take_max(i, u + 1, first_product(u, j), at[j])
                        if j in K_AT and u < UL - 1:
                            if j in KEY_MAX:
                                take_max(i, u + 1, first_product(u, j), sum(KEY_MAX[j]))
                            key_lo_part(i, last, (u + 1) * NC + K_AT[j])
                        if j - 1 in split_at(u) and u in SPLIT_OF and not last:
                            split_lo(i, last, SPLIT_OF[u], split_at(u)[j - 1])
                        if j in DIVIDE_AT and u % UL:
                            divide(i, last, u - 1, step, (DIVIDE_AT.index(j),))
                    if u == 1:
                        nc.vector.tensor_copy(bias_now[:, 1, :], bias_col[:, 1, bass.ds(i, 1), :].rearrange("p b j -> p (b j)")).then_inc(s_bnow, 1)
                    if u == UL + 1 and not last:
                        dve.wait_ge(s_exp, i * N_SC + UL * J)
                        nc.vector.tensor_copy(bias_now[:, 0, :], bias_col[:, 0, bass.ds(i + 1, 1), :].rearrange("p b j -> p (b j)")).then_inc(s_bnow, 1)
                    if u == UL - 1:
                        between_layers(i, last, step)
                if last:
                    invert(i, last, U - 1)
                    divide(i, last, U - 1, step)
                    finish(i, last)
                else:
                    for n in range(PARTS):
                        split_lo(i, last, LOADS - 1, n)
                    invert(i, last, U - 1)
                    divide(i, last, U - 1, step)
                    key_lo_part(i, last, 0)
                    finish(i, last)
                    take_max(i, U, 0, PAIRS)
                    for n in range(1, NC):
                        key_lo_part(i, last, n)
                        take_max(i, U, n * PAIRS, PAIRS)
                assert step.n == DVE_STEPS, step.n

            def between_layers(i, last, step):
                if not last:
                    for n in range(PARTS):
                        split_lo(i, last, 1, n)
                invert(i, last, UL - 1)
                divide(i, last, UL - 1, step)
                dve.wait_ge(s_resid, i + 1)
                dve.wait_ge(s_job, banks.done(i, last, ("out", 0)))
                nc.vector.tensor_tensor(resid[:, :], job_ps[banks.slot(i, last, ("out", 0))][0:S, :], resid[:, :], ALU.add).then_inc(s_free_dve, 1)
                dve.wait_ge(s_free_dve, banks.freed(i, last, ("out", 0)))
                moments(i, 0, resid[:, :], step)
                step.inc(nc.vector.scalar_tensor_tensor(out=resid[:, :], in0=resid[:, :], scalar=mv[:, 0, 0:1], in1=g_row[:, :],
                                                        op0=ALU.subtract, op1=ALU.mult))
                step.wait()
                dve.wait_ge(s_rstd, i * 2 + 1)
                step.inc(nc.vector.scalar_tensor_tensor(out=resid[:, :], in0=resid[:, :], scalar=rstd[:, 0, :], in1=b_row[:, :],
                                                        op0=ALU.mult, op1=ALU.add))
                step.wait()
                moments(i, 1, resid[:, :], step)
                dve.wait_ge(s_rstd, i * 2 + 2)
                nc.vector.tensor_scalar(norm, resid[:, :], mv[:, 1, 0:1], rstd[:, 1, :], ALU.subtract, ALU.mult).then_inc(s_norm, 1)
                if not last:
                    for n in range(PARTS):
                        split_lo(i, last, 2, n)
                dve.wait_ge(s_job, banks.done(i, last, ("z", 0)))
                bank = job_ps[banks.slot(i, last, ("z", 0))][:, 0:KT * S].rearrange("p (k s) -> p k s", k=KT)
                nc.vector.tensor_tensor(zT[:, :, :], bank, cols[:, 3, :].unsqueeze(2).to_broadcast([P, KT, S]), ALU.mult).then_inc(s_free_dve, 1)
                dve.wait_ge(s_free_dve, banks.freed(i, last, ("z", 0)))
                nc.vector.tensor_tensor(zT[:, :, :], zT[:, :, :], cols[:, 4, :].unsqueeze(2).to_broadcast([P, KT, S]), ALU.add).then_inc(s_zT, 1)
                dve.wait_ge(s_blk, i * U * 2 + UL * 2)
                dve.wait_ge(s_job, banks.done(i, last, ("Q1", 0)))
                bank = job_ps[banks.slot(i, last, ("Q1", 0))][:, 0:KT * S].rearrange("p (k s) -> p k s", k=KT)
                nc.vector.tensor_scalar(q_hi[:, :, :], bank, SCALE, None, ALU.mult).then_inc(s_q, 1)
                dve.wait_ge(s_q, i * 3 + 3)
                nc.vector.scalar_tensor_tensor(out=q_lo[:, :, :], in0=bank, scalar=SCALE, in1=q_hi[:, :, :].bitcast(F32),
                                               op0=ALU.mult, op1=ALU.subtract).then_inc(s_free_dve, 1)
                take_max(i, UL, 0, N_UNIT)

            def finish(i, last):
                dve.wait_ge(s_job, banks.done(i, last, ("out", 1)))
                nc.vector.tensor_tensor(resid[:, :], job_ps[banks.slot(i, last, ("out", 1))][0:S, :], resid[:, :], ALU.add).then_inc(s_free_dve, 1)

            with dve.Fori(0, B - 1) as i:
                batch(i, False)
            batch(B - 1, True)

        @block.gpsimd
        def _(pool):
            def spread_queries(i, last, u):
                ct = u % UL
                shape = [P, HU, S]
                m = hmask[:, :].unsqueeze(2).to_broadcast(shape)
                if UL <= u < U:
                    pool.wait_ge(s_free_dve, banks.freed(i, last, ("Q1", 0)))
                else:
                    pool.wait_ge(s_q, i * 3 + (2 if u < UL else 5))
                if u >= 2:
                    pool.wait_ge(s_score, i * N_SC + (u - 1) * J)
                nc.gpsimd.tensor_tensor(blk_hi[:, par(u), :, :], q_hi[:, ct, :].bitcast(F32).unsqueeze(1).to_broadcast(shape), m, ALU.mult).then_inc(s_blk, 1)
                nc.gpsimd.tensor_tensor(blk_lo[:, par(u), :, :], q_lo[:, ct, :].unsqueeze(1).to_broadcast(shape), m, ALU.mult).then_inc(s_blk, 1)

            def spread_max(i, u):
                if u:
                    pool.wait_ge(s_score, i * N_SC + ((u - 1) * J + TENSOR_TILES[(u - 1) // UL]))
                pool.wait_ge(s_rowmax, i * U + (u + 1))
                shape = [PW, PAIRS, PW]
                nc.gpsimd.tensor_tensor(shift[:, :].rearrange("p (a c) -> p a c", a=PAIRS),
                                        ident_sb[:, :].unsqueeze(1).to_broadcast(shape),
                                        minus_max[:, par(u), :].unsqueeze(2).to_broadcast(shape), ALU.mult).then_inc(s_shift, 1)

            pool.wait_ge(s_consts, CONSTS)
            pool.wait_ge(s_fill, 3)
            pool.wait_ge(s_wk_hi, 1)
            nc.gpsimd.tensor_tensor(wk_lo[:, :, :], raw_wk, wk_hi[:, :, :].bitcast(F32), ALU.subtract).then_inc(s_wk_lo, 1)
            spread_queries(0, False, 0)
            spread_max(0, 0)
            pool.wait_ge(s_rows, 64)

            def add_up(i, last, u, j):
                n = u * J + j
                pool.wait_ge(s_exp, i * N_SC + (n + 1))
                if j == 1:
                    used = ("Q1", 0) if u == UL else ("sum", u - 1)
                    pool.wait_ge(s_job, banks.done(i, last, used) if u else banks.done_ahead(i))
                    first = probs[0:TP, (n - 1) % RING * W:((n - 1) % RING + 1) * W]
                else:
                    pool.wait_ge(s_acc, i * N_ACCS + acc_count(n - 1))
                    first = acc[0:TP, :]
                nc.gpsimd.tensor_tensor(acc[0:TP, :], first, probs[0:TP, n % RING * W:(n % RING + 1) * W], ALU.add).then_inc(s_acc, 1)

            def batch(i, last):
                for u in range(U):
                    if u != UL - 1 and u != U - 1:
                        spread_queries(i, last, u + 1)
                    if u == 0:
                        pool.wait_ge(s_x, i * 16 + 16)
                        nc.gpsimd.tensor_tensor(resid[:, :], resid[:, :], bo_row[:, :], ALU.add).then_inc(s_resid, 1)
                    for j in range(1, J - TAIL):
                        add_up(i, last, u, j)
                        if j == Q_AT and u == U - 1 and not last:
                            spread_queries(i, last, U)
                        if j == SHIFT_AT[u // UL] and u % UL != UL - 1:
                            spread_max(i, u + 1)
                    if u == UL - 1:
                        for n in range(2):
                            pool.wait_ge(s_var, i * 2 + (n + 1))
                            nc.gpsimd.tensor_tensor(rstd[:, n, :], vpe[:, n, :], minus_half[:, :], ALU.pow).then_inc(s_rstd, 1)
                        spread_queries(i, last, UL)
                        spread_max(i, UL)
                if not last:
                    spread_max(i, U)

            with pool.Fori(0, B - 1) as i:
                batch(i, False)
            batch(B - 1, True)


def kernel(x, ctx_4096, mask_BxS2_ik0, mask_BxS2_bf1, L0_xattn_Wq, L0_xattn_bq, L0_xattn_Wk, L0_xattn_bk,
           L0_xattn_Wv, L0_xattn_bv, L0_xattn_Wo, L0_xattn_bo, L0_xattn_ln_g, L0_xattn_ln_b,
           L1_xattn_Wq, L1_xattn_Wout, L1_xattn_ln_gamma, L1_xattn_ln_beta):
    import numpy as np
    import concourse.bacc as bacc
    from concourse.bass_utils import run_bass_kernel_spmd

    x, ctx = np.asarray(x), np.asarray(ctx_4096)
    mask0 = np.asarray(mask_BxS2_ik0)
    mask1 = np.asarray(mask_BxS2_bf1).view(np.uint8)
    by_channel = lambda v: np.ascontiguousarray(np.asarray(v).reshape(KT, P).T)
    turned = lambda w: np.ascontiguousarray(np.asarray(w).T)
    positions = lambda m: np.ascontiguousarray(m.reshape(B, TP, J).transpose(1, 0, 2).reshape(TP, B * J))
    heads = np.arange(P)[:, None] // HD == np.arange(HU)[None, :]
    halves = (np.arange(P)[:, None] // HD) % 2 == np.arange(2)[None, :]
    arrays = {
        "x": x,
        "xT": turned(x.reshape(B * S, H)),
        "ctx": ctx,
        "ctxT": np.ascontiguousarray(ctx.reshape(B, TP, J, H).transpose(0, 3, 2, 1).reshape(B, H, T)),
        "mask0": positions(mask0), "mask1": positions(mask1),
        "mask0T": turned(positions(mask0)), "mask1T": turned(positions(mask1)),
        "Wq0T": turned(L0_xattn_Wq), "bq": by_channel(L0_xattn_bq),
        "Wk0T": turned(L0_xattn_Wk), "bk": by_channel(L0_xattn_bk),
        "Wv0T": turned(L0_xattn_Wv), "bv": by_channel(L0_xattn_bv),
        "Wo0T": turned(L0_xattn_Wo), "bo": np.asarray(L0_xattn_bo),
        "ln_g": np.asarray(L0_xattn_ln_g), "ln_b": np.asarray(L0_xattn_ln_b),
        "Wq1T": turned(L1_xattn_Wq), "Wo1T": turned(L1_xattn_Wout),
        "gamma": by_channel(L1_xattn_ln_gamma), "beta": by_channel(L1_xattn_ln_beta),
        "ident": np.eye(PW, dtype=np.float32),
        "headmask": heads.astype(np.float32), "halves": halves.astype(np.float32),
    }
    nc = bacc.Bacc("TRN2", target_bir_lowering=False, num_devices=1)
    args = {n: nc.dram_tensor(f"in_{n}_dram", a.shape, mybir.dt.from_np(a.dtype), kind="ExternalInput").ap() for n, a in arrays.items()}
    args["out"] = nc.dram_tensor("out_dram", (B, S, H), F32, kind="ExternalOutput").ap()
    cross_attention(nc, **args)
    r = run_bass_kernel_spmd(nc, [{f"in_{n}_dram": a for n, a in arrays.items()}], core_ids=[0])
    return r.results[0]["out_dram"]
```
